# Optimizing a Trainium2 kernel written in Bass

```python
import numpy as np
import jax
import jax.numpy as jnp

def _softmax(x, axis=-1):
    return jax.nn.softmax(x, axis=axis)

def _gelu(x):
    return jax.nn.gelu(x, approximate=True)

def _silu(x):
    return jax.nn.silu(x)

def _sigmoid(x):
    return jax.nn.sigmoid(x)

def _layernorm(x, axis=-1, eps=1e-05):
    m = jnp.mean(x, axis=axis, keepdims=True)
    v = jnp.var(x, axis=axis, keepdims=True)
    return (x - m) / jnp.sqrt(v + eps)

def _scatter_add(tgt, idx, src, axis=0):
    return tgt.at[idx].add(src)

def _segment_sum(src, seg, n):
    return jax.ops.segment_sum(src, seg, n)
kernel_name = 'mk_seq_preln_d1_jaxref_r8_8e1583'

def setup_inputs(seed: int=0):
    np.random.seed(seed)
    _w = jnp.asarray

    def _L0_attn_setup():
        import jax, jax.numpy as jnp
        import numpy as np
        import math
        D_MODEL = 128
        N_HEADS = 16
        HEAD_DIM = D_MODEL // N_HEADS

        def rotary_embedding(dim, seq_len):
            inv_freq = 1.0 / 10000.0 ** (jnp.arange(0, dim, 2, dtype=jnp.float32) / dim)
            t = jnp.arange(seq_len, dtype=jnp.float32)
            freqs = t[:, None] * inv_freq[None, :]
            return jnp.concatenate((freqs, freqs), axis=-1)

        def apply_rope(x, rope):
            x1 = x[..., ::2]
            x2 = x[..., 1::2]
            ang = rope[..., ::2]
            c, s = (jnp.cos(ang), jnp.sin(ang))
            o1 = x1 * c - x2 * s
            o2 = x1 * s + x2 * c
            return jnp.stack((o1, o2), axis=-1).reshape(x.shape)
        key = jax.random.key(seed)
        ks = jax.random.split(key, 9)
        d = D_MODEL
        sc = 1.0 / math.sqrt(d)
        return {'x': jax.random.normal(ks[0], (2, 256, d), dtype=jnp.float32), 'Wq': jax.random.normal(ks[1], (d, d), dtype=jnp.float32) * sc, 'bq': jax.random.normal(ks[2], (d,), dtype=jnp.float32) * 0.02, 'Wk': jax.random.normal(ks[3], (d, d), dtype=jnp.float32) * sc, 'bk': jax.random.normal(ks[4], (d,), dtype=jnp.float32) * 0.02, 'Wv': jax.random.normal(ks[5], (d, d), dtype=jnp.float32) * sc, 'bv': jax.random.normal(ks[6], (d,), dtype=jnp.float32) * 0.02, 'Wo': jax.random.normal(ks[7], (d, d), dtype=jnp.float32) * sc, 'bo': jax.random.normal(ks[8], (d,), dtype=jnp.float32) * 0.02}
    _L0_attn_in = _L0_attn_setup()

    def _L0_ffn_setup():
        import jax, jax.numpy as jnp
        import numpy as np
        D_MODEL, FF_DIM = (128, 256)
        N_SHARED, N_ROUTED, TOP_K = (1, 8, 2)
        BATCH, SEQ = (2, 256)
        key = jax.random.key(seed)
        ks = jax.random.split(key, 8)
        init = lambda k, shape: jax.random.normal(k, shape, jnp.float32) * 0.02
        x = jax.random.normal(ks[0], (BATCH, SEQ, D_MODEL), jnp.float32)
        Wg = init(ks[1], (D_MODEL, N_ROUTED))
        Ws1 = init(ks[2], (D_MODEL, FF_DIM))
        Ws3 = init(ks[3], (D_MODEL, FF_DIM))
        Ws2 = init(ks[4], (FF_DIM, D_MODEL))
        We1 = init(ks[5], (N_ROUTED, D_MODEL, FF_DIM))
        We3 = init(ks[6], (N_ROUTED, D_MODEL, FF_DIM))
        We2 = init(ks[7], (N_ROUTED, FF_DIM, D_MODEL))
        return {'x': x, 'Wg': Wg, 'Ws1': Ws1, 'Ws3': Ws3, 'Ws2': Ws2, 'We1': We1, 'We3': We3, 'We2': We2}
    _L0_ffn_in = _L0_ffn_setup()
    _d = {'L0_attn_x': _L0_attn_in['x'], 'L0_attn_Wq': _L0_attn_in['Wq'], 'L0_attn_bq': _L0_attn_in['bq'], 'L0_attn_Wk': _L0_attn_in['Wk'], 'L0_attn_bk': _L0_attn_in['bk'], 'L0_attn_Wv': _L0_attn_in['Wv'], 'L0_attn_bv': _L0_attn_in['bv'], 'L0_attn_Wo': _L0_attn_in['Wo'], 'L0_attn_bo': _L0_attn_in['bo'], 'L0_ffn_Wg': _L0_ffn_in['Wg'], 'L0_ffn_Ws1': _L0_ffn_in['Ws1'], 'L0_ffn_Ws3': _L0_ffn_in['Ws3'], 'L0_ffn_Ws2': _L0_ffn_in['Ws2'], 'L0_ffn_We1': _L0_ffn_in['We1'], 'L0_ffn_We3': _L0_ffn_in['We3'], 'L0_ffn_We2': _L0_ffn_in['We2']}
    _x0 = _d['L0_attn_x']
    _d['L0_attn_x'] = jax.random.normal(jax.random.fold_in(jax.random.key(seed), 1), (16, 256, 128), dtype=_x0.dtype)
    del _x0
    return _d

def reference(L0_attn_x, L0_attn_Wq, L0_attn_bq, L0_attn_Wk, L0_attn_bk, L0_attn_Wv, L0_attn_bv, L0_attn_Wo, L0_attn_bo, L0_ffn_Wg, L0_ffn_Ws1, L0_ffn_Ws3, L0_ffn_Ws2, L0_ffn_We1, L0_ffn_We3, L0_ffn_We2):

    def _L0_attn_ref(x, Wq, bq, Wk, bk, Wv, bv, Wo, bo):
        import jax, jax.numpy as jnp
        import numpy as np
        import math
        D_MODEL = 128
        N_HEADS = 16
        HEAD_DIM = D_MODEL // N_HEADS

        def rotary_embedding(dim, seq_len):
            inv_freq = 1.0 / 10000.0 ** (jnp.arange(0, dim, 2, dtype=jnp.float32) / dim)
            t = jnp.arange(seq_len, dtype=jnp.float32)
            freqs = t[:, None] * inv_freq[None, :]
            return jnp.concatenate((freqs, freqs), axis=-1)

        def apply_rope(x, rope):
            x1 = x[..., ::2]
            x2 = x[..., 1::2]
            ang = rope[..., ::2]
            c, s = (jnp.cos(ang), jnp.sin(ang))
            o1 = x1 * c - x2 * s
            o2 = x1 * s + x2 * c
            return jnp.stack((o1, o2), axis=-1).reshape(x.shape)
        B, S, d = x.shape
        H, Dh = (N_HEADS, HEAD_DIM)
        q = (x @ Wq + bq).reshape(B, S, H, Dh).transpose(0, 2, 1, 3)
        k = (x @ Wk + bk).reshape(B, S, H, Dh).transpose(0, 2, 1, 3)
        v = (x @ Wv + bv).reshape(B, S, H, Dh).transpose(0, 2, 1, 3)
        rope = rotary_embedding(Dh, S)
        q = apply_rope(q, rope)
        k = apply_rope(k, rope)
        scores = jnp.einsum('bhqd,bhkd->bhqk', q, k) / math.sqrt(Dh)
        attn = jax.nn.softmax(scores, axis=-1)
        out = jnp.einsum('bhqk,bhkd->bhqd', attn, v)
        out = out.transpose(0, 2, 1, 3).reshape(B, S, d)
        return out @ Wo + bo

    def _L0_ffn_ref(x, Wg, Ws1, Ws3, Ws2, We1, We3, We2):
        import jax, jax.numpy as jnp
        import numpy as np
        D_MODEL, FF_DIM = (128, 256)
        N_SHARED, N_ROUTED, TOP_K = (1, 8, 2)
        BATCH, SEQ = (2, 256)
        B, S, d = x.shape
        E = Wg.shape[1]
        xf = x.reshape(-1, d)
        T = xf.shape[0]
        gates = jax.nn.sigmoid(xf @ Wg)
        vals, idx = jax.lax.top_k(gates, TOP_K)
        vals = vals / vals.sum(axis=-1, keepdims=True)
        w = jnp.zeros((T, E), x.dtype).at[jnp.arange(T)[:, None], idx].add(vals)
        shared = jax.nn.silu(xf @ Ws1) * (xf @ Ws3) @ Ws2
        h = jax.nn.silu(jnp.einsum('td,edf->tef', xf, We1)) * jnp.einsum('td,edf->tef', xf, We3)
        routed = jnp.einsum('tef,efd,te->td', h, We2, w)
        out = (shared + routed) / (N_SHARED + TOP_K)
        return out.reshape(B, S, d)
    x = L0_attn_x
    x = x + _L0_attn_ref(_layernorm(x, axis=-1), L0_attn_Wq, L0_attn_bq, L0_attn_Wk, L0_attn_bk, L0_attn_Wv, L0_attn_bv, L0_attn_Wo, L0_attn_bo)
    x = x + _L0_ffn_ref(_layernorm(x, axis=-1), L0_ffn_Wg, L0_ffn_Ws1, L0_ffn_Ws3, L0_ffn_Ws2, L0_ffn_We1, L0_ffn_We3, L0_ffn_We2)
    return x

_drawn_inputs = setup_inputs


def setup_inputs(seed=0):
    import zlib

    import numpy as np

    out = dict(_drawn_inputs(seed))
    spreads = {}
    factors = {'L0_attn_bq': 8.0,
     'L0_attn_bk': 8.0,
     'L0_attn_bo': 2.721,
     'L0_ffn_Wg': 8.0,
     'L0_ffn_Ws1': 8.0,
     'L0_ffn_Ws3': 8.0,
     'L0_ffn_Ws2': 8.0,
     'L0_ffn_We1': 8.0,
     'L0_ffn_We3': 8.0,
     'L0_ffn_We2': 8.0}
    for name, (base, spread) in spreads.items():
        noise = np.random.default_rng([zlib.crc32(name.encode()), seed]).standard_normal(out[name].shape)
        drawn = base * np.exp(spread * noise) if base else spread * noise
        out[name] = jnp.asarray(drawn.astype(out[name].dtype))
    for name, factor in factors.items():
        out[name] = (out[name] * factor).astype(out[name].dtype)
    return out
```

```python
from contextlib import ExitStack

import concourse.bass as bass
from concourse import mybir

ALU = mybir.AluOpType
ACT = mybir.ActivationFunctionType
AX = mybir.AxisListType
F32 = mybir.dt.float32
F32R = mybir.dt.float32r

P = 128
NB = 16
S = 256
D = 128
H = 16
DH = 8
G = 4
J = 4
TT = S // P
NT = NB * TT
F = 256
FH = F // P
NE = 8
NEX = NE + 1
CH = 512
NCH = NB * S // CH
CT = CH // P
KA = 96
KB = 104
NBUF = 3
SCALE = float(DH) ** -0.5
EPS = 1e-5

C_ROPE = 0
C_IDENT = C_ROPE + 2 * S
C_MASK = C_IDENT + P
C_ALL = C_MASK + J


def layer_kernel(nc, x, w_att, b_cols, bv, bo, Wg, w_up, w_down, const, out):
    with ExitStack() as ctx:
        def sb(name, shape, dt=F32):
            return ctx.enter_context(nc.sbuf_tensor(name, shape, dt))

        def sem(name):
            return ctx.enter_context(nc.semaphore(name))

        X = sb("X", [P, NT, D])
        cst = sb("cst", [P, C_ALL])
        wraw = sb("wraw", [P, 6, D])
        wg = sb("wg", [P, NE])
        bcol = sb("bcol", [P, 4])
        brow = sb("brow", [P, 2, D])
        stat = sb("stat", [P, TT, 6])
        mv = sb("mv", [P, TT, 2])
        veps = sb("veps", [P, TT])
        rstd = sb("rstd", [P, TT])
        halves = sb("halves", [P, TT])
        stat2 = sb("stat2", [P, TT, 6])
        mv2 = sb("mv2", [P, TT, 2])
        veps2 = sb("veps2", [P, TT])
        rstd2 = sb("rstd2", [P, TT])
        xn = sb("xn", [P, TT, D])
        xn2 = sb("xn2", [P, TT, D])
        xnT = sb("xnT", [P, S])
        rc = sb("rc", [P, 2, S])
        rs = sb("rs", [P, 2, S])
        HL = sb("HL", [P, 2, 2, S], F32R)
        QK = sb("QK", [P, NBUF, 2, G, S], F32R)
        KZ = sb("KZ", [P, NBUF, G, J, S], F32R)
        VX = sb("VX", [P, NBUF, TT, H, 32])
        MX = sb("MX", [P, TT, H])
        MHL = sb("MHL", [P, TT, G, 2, J], F32R)
        MT = sb("MT", [32, S], F32R)
        PR = sb("PR", [P, 8, TT, S])
        UT = sb("UT", [P, G, S])
        rden = sb("rden", [P, TT, H])
        att = sb("att", [P, TT, D])
        attT = sb("attT", [P, S])
        xf = sb("xf", [P, S])
        XH = sb("XH", [P, NB * S], F32R)
        XL = sb("XL", [P, NB * S], F32R)
        GE = sb("GE", [P, NT, NE])
        WHL = sb("WHL", [P, NT, 2, NE], F32R)
        WC = sb("WC", [P, CT, 2 * NE])
        up_raw = sb("up_raw", [P, NEX, 2 * F])
        dn_raw = sb("dn_raw", [P, NEX, FH, D])
        kz_flat = KZ[:, :, :, :, :].rearrange("p n g j t -> p (n g j t)")
        qk_flat = QK[:, :, :, :, :].rearrange("p n a g t -> p (n a g t)")
        UPW, DNW = NEX * 2 * F, NEX * FH * D
        w_up_part = [kz_flat[:, l * UPW:(l + 1) * UPW].rearrange("p (e f) -> p e f", e=NEX) for l in range(2)]
        w_dn_part = [qk_flat[:, l * DNW:(l + 1) * DNW].rearrange("p (e v d) -> p e v d", e=NEX, v=FH)
                     for l in range(2)]
        hid_part = kz_flat[:, 2 * UPW:2 * UPW + 3 * 2 * CH].rearrange("p (n l t) -> p n l t", n=3, l=2)
        SEL = qk_flat[0:2 * NE, 2 * DNW:2 * DNW + NE * P].rearrange("p (e m) -> p e m", e=NE)
        WT = qk_flat[0:2 * NE, 2 * DNW + NE * P:2 * DNW + NE * P + CH]
        work = PR[:, :, :, :].rearrange("p n a t -> p n (a t)")
        silu, silw, hid, wrow = work[:, 0:2, :], work[:, 2:4, :], work[:, 4:6, :], work[:, 6:8, :]
        yT = UT[:, :, :].rearrange("p g t -> p (g t)")[:, 0:CH]
        vx_flat = VX[:, :, :, :, :].rearrange("p n a h c -> p (n a h c)")

        def rtile(n, width=NE):
            return vx_flat[:, n * NT * NE:n * NT * NE + NT * width].rearrange("p (t e) -> p t e", t=NT)

        gate, rank, wsel, wpart = rtile(0), rtile(1), rtile(2), rtile(3)
        beats = vx_flat[:, 4 * NT * NE:12 * NT * NE].rearrange("p (t e j) -> p t e j", t=NT, e=NE)
        wsum, wrec = GE[:, :, 0:1], GE[:, :, 1:2]
        ps = ctx.enter_context(nc.psum_tensor("ps", [P, 8, 512], F32))
        SA, SB, PU, PM = 0, 2, 5, 6

        ld = sem("ld")
        wld = sem("wld")
        xld = [sem(f"xld{n}") for n in range(4)]
        setup_dve = sem("setup_dve")
        setup_pool = sem("setup_pool")
        ve1 = sem("ve1"); ve2 = sem("ve2"); st1 = sem("st1"); mv1 = sem("mv1"); rs1 = sem("rs1")
        st2 = sem("st2"); mvs2 = sem("mvs2"); rs2 = sem("rs2")
        xn_ok = sem("xn_ok")
        xn2_ok = sem("xn2_ok")
        xt_ok = sem("xt_ok")
        xnT_ok = sem("xnT_ok")
        q_ok = sem("q_ok"); k_ok = sem("k_ok"); v_ok = sem("v_ok")
        rq_ok = sem("rq_ok"); rk_ok = sem("rk_ok")
        vx_ok = sem("vx_ok")
        bo_ok = sem("bo_ok")
        rot_ok = sem("rot_ok"); hi_ok = sem("hi_ok"); lo_ok = sem("lo_ok")
        qk_ok = [sem(f"qk_ok{g}") for g in range(G)]
        kz_ok = sem("kz_ok")
        sa_ok = sem("sa_ok")
        mx_ok = sem("mx_ok")
        mh_ok = sem("mh_ok"); ml_ok = sem("ml_ok")
        mt_ok = sem("mt_ok")
        mts_ok = sem("mts_ok")
        sh_ok = [sem(f"sh_ok{g}") for g in range(G)]
        sb_ok = sem("sb_ok")
        ex_ok = sem("ex_ok")
        pv_ok = sem("pv_ok")
        ut_ok = sem("ut_ok")
        un_ok = sem("un_ok")
        rd_ok = sem("rd_ok")
        att_ok = sem("att_ok")
        at_ok = sem("at_ok")
        atT_ok = sem("atT_ok")
        wo_ok = sem("wo_ok")
        x2_ok = sem("x2_ok")
        xt2_ok = sem("xt2_ok"); xf_ok = sem("xf_ok"); xh_ok = sem("xh_ok"); xl_ok = sem("xl_ok")
        g_ok = sem("g_ok")
        ge_ok = sem("ge_ok")

        wh_ok = sem("wh_ok"); wl_ok = sem("wl_ok")
        sel_ok = sem("sel_ok")
        rt = sem("rt")
        wc_ok = sem("wc_ok"); wt_t = sem("wt_t"); wt_ok = sem("wt_ok")
        wb_t = sem("wb_t"); wb_ok = sem("wb_ok")
        gu_ok = sem("gu_ok")
        si_ok = sem("si_ok")
        sw_ok = sem("sw_ok")
        h_ok = sem("h_ok"); hh_ok = sem("hh_ok"); hl_ok = sem("hl_ok")
        dn_ok = sem("dn_ok")
        yT_ok = sem("yT_ok"); y_t = sem("y_t"); y_ok = sem("y_ok")
        out_ok = sem("out_ok")

        HV = NEX * FH
        G0, U0, Y0, M0 = 0, 2, 4, 5

        rope = cst[:, C_ROPE:C_ROPE + 2 * S].rearrange("p (a t) -> p a t", a=2)
        ident = cst[:, C_IDENT:C_IDENT + P]

        def mask(j):
            return cst[:, C_MASK + j:C_MASK + j + 1]

        x_v = x.rearrange("b (a p) d -> p (b a) d", p=P)
        out_v = out.rearrange("b (a p) d -> p (b a) d", p=P)
        XLOADS = (0, 2, 4, 16, NT)
        NLD = 6
        STACKS = 3

        def wrow_bank(e):
            return M0 + (e % 2 if e < 3 else (e + 1) % 2)

        def tiles(b):
            return bass.ds(b * TT, TT)

        def stages(i):
            return (0 <= i + 2 < NB, 0 <= i + 1 < NB, 0 <= i < NB, 0 <= i - 1 < NB, 0 <= i - 2 < NB)

        def run(eng, iteration):
            first = NBUF - 1
            turns = (NB - 3 - first) // NBUF
            for i in range(-2, first):
                iteration(i, i % NBUF, stages(i), i)
            with eng.Fori(first, first + (turns - 1) * NBUF + 1, NBUF) as base:
                for r in range(NBUF):
                    iteration(base + r, (first + r) % NBUF, (True,) * 5, first)
            for i in range(first + turns * NBUF, NB + 2):
                iteration(i, i % NBUF, stages(i), i)

        block = ctx.enter_context(nc.Block())

        @block.sync
        def _(sp):
            for n, (lo, hi) in enumerate(zip(XLOADS, XLOADS[1:])):
                sp.dma_start(X[:, lo:hi, :], x_v[:, lo:hi, :]).then_inc(xld[n], 16)
                if n == 0:
                    sp.dma_start(cst[:, :], const).then_inc(ld, 16)
                    sp.dma_start(wraw[:, :, :], w_att.rearrange("p (n d) -> p n d", n=6)).then_inc(ld, 16)
            sp.dma_start(wg[:, :], Wg).then_inc(ld, 16)
            sp.dma_start(bcol[:, :], b_cols).then_inc(ld, 16)
            for n, b in enumerate((bv, bo)):
                sp.dma_start(brow[:, n, :], b.rearrange("(o d) -> o d", o=1).broadcast_to([P, D])).then_inc(ld, 16)

            sp.dma_start(up_raw[:, :, :], w_up).then_inc(wld, 16)
            sp.dma_start(dn_raw[:, :, :, :], w_down).then_inc(wld, 16)

            def iteration(i, ph, has, _):
                front, _, scores, _, _ = has
                if scores:
                    sp.wait_ge(mts_ok, i + 1)
                    for g in range(G):
                        sp.dma_start(QK[KA:KB, ph, 0, g, :].bitcast(F32), MT[8 * g:8 * g + 8, :].bitcast(F32)).then_inc(sh_ok[g], 16)
                if front:
                    f, pf = i + 2, (ph + 2) % NBUF
                    sp.wait_ge(lo_ok, f + 1)
                    flat = HL[:, :, :, :].rearrange("p a b t -> p (a b) t")
                    for g in range(G):
                        for r, (q, k) in enumerate(((0, 2), (1, 2), (0, 3))):
                            sp.dma_start(QK[32 * r:32 * r + 32, pf, :, g, :].bitcast(F32),
                                         flat[32 * g:32 * g + 32, q:k + 1:k - q, :].bitcast(F32)).then_inc(qk_ok[g], 16)

            run(sp, iteration)

            def store(c):
                sp.wait_ge(y_ok, c + 1)
                sp.dma_start(out_v[:, bass.ds(c * CT, CT), :], X[:, bass.ds(c * CT, CT), :]).then_inc(out_ok, 16)

            with sp.Fori(0, NCH, 1) as c:
                store(c)
            sp.wait_ge(out_ok, 16 * NCH)

        @block.gpsimd
        def _(pool):
            pool.memset(VX[:, :, :, :, :], 0.0).then_inc(setup_pool, 1)
            pool.wait_ge(setup_pool, 1)
            pool.memset(VX[:, :, :, :, DH:DH + 1], 1.0).then_inc(setup_pool, 1)
            pool.wait_ge(setup_dve, NBUF + 1)

            def root(b, v, r, ready, done):
                pool.wait_ge(ready, b + 1)
                pool.tensor_tensor(r[:, :], v[:, :], halves[:, :], op=ALU.pow).then_inc(done, 1)

            root(0, veps, rstd, ve1, rs1)
            pool.wait_ge(ld, 16 * NLD)

            def iteration(i, ph, has, _):
                front, _, _, _, gates = has
                if gates:
                    root(i - 2, veps2, rstd2, ve2, rs2)
                if front:
                    f, pf = i + 2, (ph + 2) % NBUF
                    pool.wait_ge(xn_ok, f + 1)
                    pool.tensor_tensor(X[:, tiles(f), :], X[:, tiles(f), :],
                                       brow[:, 1:2, :].broadcast_to([P, TT, D]), op=ALU.add).then_inc(bo_ok, 1)
                    pool.wait_ge(rk_ok, f + 1)
                    pool.wait_ge(rq_ok, f + 1)
                    pool.tensor_tensor(rc[:, :, :], rc[:, :, :], rs[:, :, :], op=ALU.add).then_inc(rot_ok, 1)
                    pool.wait_ge(hi_ok, f + 1)
                    pool.tensor_tensor(HL[:, :, 1, :], rc[:, :, :], HL[:, :, 0, :].bitcast(F32),
                                       op=ALU.subtract).then_inc(lo_ok, 1)
                if gates:
                    t = i - 2
                    pool.wait_ge(xh_ok, t + 1)
                    tok = bass.ds(t * S, S)
                    pool.tensor_tensor(XL[:, tok], xf[:, :], XH[:, tok].bitcast(F32),
                                       op=ALU.subtract).then_inc(xl_ok, 1)
                if front:
                    if not isinstance(i, int) or i + 3 < NB:
                        root(i + 3, veps, rstd, ve1, rs1)
                    for g in range(G):
                        pool.wait_ge(qk_ok[g], 16 * STACKS * (f + 1))
                        pool.tensor_tensor(KZ[:, pf, g, 0, :], QK[:, pf, 1, g, :].bitcast(F32),
                                           mask(0).broadcast_to([P, S]), op=ALU.mult)
                        for j in range(1, J):
                            last = pool.tensor_scalar(KZ[:, pf, g, j, :], QK[:, pf, 1, g, :].bitcast(F32),
                                                      mask(j), 1.0, ALU.mult, ALU.mult)
                        last.then_inc(kz_ok, 1)

            run(pool, iteration)

            pool.wait_ge(sb_ok, NB * H)
            for e in range(NEX):
                pool.wait_ge(wh_ok, e + 1)
                pool.tensor_tensor(w_up_part[1][:, e, :], up_raw[:, e, :], w_up_part[0][:, e, :].bitcast(F32),
                                   op=ALU.subtract)
                pool.tensor_tensor(w_dn_part[1][:, e, :, :], dn_raw[:, e, :, :],
                                   w_dn_part[0][:, e, :, :].bitcast(F32), op=ALU.subtract).then_inc(wl_ok, 1)

            def chunk(c):
                for q in range(FH, HV):
                    e = q // FH
                    pool.wait_ge(h_ok, c * HV + q - 1)
                    pool.wait_ge(wb_ok, c * NE + e)
                    pool.wait_ge(si_ok, c * HV + q + 1)
                    pool.tensor_tensor(silw[:, q % 2, :], silu[:, q % 2, :], wrow[:, (e - 1) % 2, :],
                                       op=ALU.mult).then_inc(sw_ok, 1)

            chunk(0)
            with pool.Fori(1, NCH, 1) as c:
                chunk(c)

        @block.scalar
        def _(act):
            def evac_heads(b, half):
                act.wait_ge(pv_ok, b * G + 2 * half + 2)
                if half == 0 and (not isinstance(b, int) or b >= 1):
                    act.wait_ge(un_ok, b * TT)
                act.activation(UT[:, 2 * half:2 * half + 2, :], ps[:, PU, :].rearrange("p (g t) -> p g t", g=2),
                               ACT.Copy).then_inc(ut_ok, 1)

            def iteration(i, ph, has, _):
                front, _, scores, tail, gates = has
                if tail:
                    evac_heads(i - 1, 1)
                if front:
                    f = i + 2
                    act.wait_ge(xt_ok, f + 1)
                    if not isinstance(i, int) or f >= 1:
                        act.wait_ge(v_ok, f)
                    act.activation(xnT[:, :], ps[:, PM + 1, 0:S], ACT.Copy).then_inc(xnT_ok, 1)
                side = []

                def hi_part():
                    f = i + 2
                    act.wait_ge(rot_ok, f + 1)
                    if not isinstance(i, int) or f >= 1:
                        for g in range(G):
                            act.wait_ge(qk_ok[g], 16 * STACKS * f)
                    act.activation(HL[:, :, 0, :], rc[:, :, :], ACT.Copy).then_inc(hi_ok, 1)

                def second_norm():
                    t = i - 2
                    act.wait_ge(xt2_ok, t + 1)
                    if not isinstance(i, int) or t >= 1:
                        act.wait_ge(xl_ok, t)
                    act.activation(xf[:, :], ps[:, PM + 1, 0:S], ACT.Copy).then_inc(xf_ok, 1)
                    act.wait_ge(xf_ok, t + 1)
                    act.activation(XH[:, bass.ds(t * S, S)], xf[:, :], ACT.Copy).then_inc(xh_ok, 1)

                def gate_exp():
                    t = i - 2
                    act.wait_ge(g_ok, t + 1)
                    act.activation(GE[:, tiles(t), :], ps[:, PM, 0:TT * NE].rearrange("p (a e) -> p a e", a=TT),
                                   ACT.Exp, scale=-1.0).then_inc(ge_ok, 1)

                def att_evac():
                    t = i - 1
                    act.wait_ge(at_ok, t + 1)
                    act.activation(attT[:, :], ps[:, PM + 1, 0:S], ACT.Copy).then_inc(atT_ok, 1)

                after = {}
                if front:
                    after[4] = hi_part
                if gates:
                    after[5] = second_norm
                    after[7] = gate_exp
                if tail:
                    after[11] = att_evac
                for h in range(H):
                    if scores:
                        n = i * H + h
                        act.wait_ge(sb_ok, n + 1)
                        if h % G == 0 and (not isinstance(i, int) or H * i + h >= 8):
                            act.wait_ge(pv_ok, i * G + h // G - 1)
                        act.activation(PR[:, h % 8, :, :],
                                       ps[:, SB + (ph + h) % 3, :].rearrange("p (a t) -> p a t", a=TT),
                                       ACT.Exp, scale=SCALE).then_inc(ex_ok, 1)
                        if h == 9:
                            evac_heads(i, 0)
                    if h in after:
                        after[h]()

            run(act, iteration)

            act.wait_ge(sb_ok, NB * H)
            act.wait_ge(kz_ok, NB * G)
            act.wait_ge(wld, 32)
            for e in range(NEX):
                act.activation(w_up_part[0][:, e, :], up_raw[:, e, :], ACT.Copy)
                act.activation(w_dn_part[0][:, e, :, :], dn_raw[:, e, :, :], ACT.Copy).then_inc(wh_ok, 1)
            act.wait_ge(pv_ok, NB * G)
            act.wait_ge(un_ok, NB * TT)

            def hidden_hi(n, q):
                if not isinstance(n, int) or n >= 3:
                    act.wait_ge(dn_ok, n - 2)
                act.wait_ge(h_ok, n + 1)
                act.activation(hid_part[:, q % 3, 0, :], hid[:, q % 2, :], ACT.Copy).then_inc(hh_ok, 1)

            def sum_out(c):
                if not isinstance(c, int) or c >= 1:
                    act.wait_ge(y_t, c)
                act.wait_ge(dn_ok, c * HV + HV)
                act.activation(yT, ps[:, Y0, :], ACT.Copy).then_inc(yT_ok, 1)

            def chunk(c):
                dyn = not isinstance(c, int)
                for q in range(HV):
                    n = c * HV + q
                    if dyn or n >= 2:
                        act.wait_ge(h_ok, n - 1)
                    act.wait_ge(gu_ok, n + 1)
                    act.activation(silu[:, q % 2, :], ps[:, G0 + q % 2, :], ACT.Silu).then_inc(si_ok, 1)
                    if dyn or n >= 1:
                        hidden_hi(n - 1, (q - 1) % HV)
                    if q % 2 and q // 2 < NE:
                        e = q // 2 + 1
                        m = c * NE + e
                        if dyn or m >= 3:
                            act.wait_ge(sw_ok, (m - 2) * FH)
                        act.wait_ge(wb_t, m)
                        act.activation(wrow[:, (e - 1) % 2, :], ps[:, wrow_bank(e), :], ACT.Copy).then_inc(wb_ok, 1)
                    if q == 1 and (dyn or c >= 1):
                        sum_out(c - 1)

            chunk(0)
            with act.Fori(1, NCH, 1) as c:
                chunk(c)
            hidden_hi(NCH * HV - 1, HV - 1)
            sum_out(NCH - 1)

        @block.vector
        def _(dve):
            dve.memset(halves[:, :], -0.5).then_inc(setup_dve, 1)
            for n in range(NBUF):
                dve.memset(QK[KA:P, n, 1, :, :].bitcast(F32), 1.0).then_inc(setup_dve, 1)

            def norm_stats(src, st, s_st):
                for a in range(TT):
                    last = dve.bn_stats(st[:, a, :], src[:, a, :])
                last.then_inc(s_st, 1)

            def norm_mean(b, st, m, v, s_mv, done):
                for a in range(TT):
                    last = dve.bn_aggr(m[:, a, :], st[:, a, :])
                last.then_inc(s_mv, 1)
                dve.wait_ge(s_mv, b + 1)
                dve.tensor_scalar(v[:, :], m[:, :, 1:2].rearrange("p a o -> p (a o)"), EPS, None,
                                  ALU.add).then_inc(done, 1)

            def norm_apply(src, dst, b, m, r, s_rs, done):
                dve.wait_ge(s_rs, b + 1)
                for a in range(TT):
                    last = dve.tensor_scalar(dst[:, a, :], src[:, a, :], m[:, a, 0:1], r[:, a:a + 1],
                                             ALU.subtract, ALU.mult)
                last.then_inc(done, 1)

            def first_apply(f, static):
                if not static:
                    dve.wait_ge(xt_ok, f)
                norm_apply(X[:, tiles(f), :], xn, f, mv, rstd, rs1, xn_ok)

            dve.wait_ge(xld[0], 16)
            norm_stats(X[:, tiles(0), :], stat, st1)
            dve.wait_ge(st1, 1)
            norm_mean(0, stat, mv, veps, mv1, ve1)
            first_apply(0, True)
            dve.wait_ge(ld, 16 * NLD)

            def iteration(i, ph, has, lowest):
                front, maxima, scores, tail, gates = has
                more = front and (not isinstance(i, int) or i + 3 < NB)

                def reduce(u):
                    if not maxima:
                        return
                    a = i + 1
                    if u == 0 and (not isinstance(i, int) or a >= 1):
                        dve.wait_ge(ml_ok, a)
                    dve.wait_ge(sa_ok, a * H + u + 1)
                    hp, qt = u // 2, u % 2
                    dve.tensor_reduce(MX[:, qt, 2 * hp:2 * hp + 2],
                                      ps[:, SA + u % 2, :].rearrange("p (h k) -> p h k", h=2),
                                      op=ALU.max, axis=AX.X).then_inc(mx_ok, 1)

                def rope_mul(n, wait, bank_, done):
                    f = i + 2
                    dve.wait_ge(wait, f + 1)
                    if n == 0 and (not isinstance(i, int) or f >= 1):
                        dve.wait_ge(lo_ok, f)
                    dve.scalar_tensor_tensor(rc[:, n, :], ps[:, PM + bank_, 0:S], bcol[:, 2 * n:2 * n + 1],
                                             rope[:, 0, :], op0=ALU.add, op1=ALU.mult)
                    dve.scalar_tensor_tensor(rs[:, n, :], ps[:, PM + bank_, S:2 * S], bcol[:, 2 * n + 1:2 * n + 2],
                                             rope[:, 1, :], op0=ALU.add, op1=ALU.mult).then_inc(done, 1)

                def values():
                    f, pf = i + 2, (ph + 2) % NBUF
                    dve.wait_ge(v_ok, f + 1)
                    if not isinstance(i, int) or i >= 1:
                        dve.wait_ge(pv_ok, i * G)
                    dve.tensor_tensor(VX[:, pf, :, :, 0:DH],
                                      ps[:, PM, 0:S].rearrange("p (a h d) -> p a h d", a=TT, h=H),
                                      brow[:, 0:1, :].rearrange("p o (h d) -> p o h d", h=H)
                                      .broadcast_to([P, TT, H, DH]), op=ALU.add).then_inc(vx_ok, 1)

                def normalise(a):
                    t = i - 1
                    bk_ = PM + 1 - a
                    u = ps[:, bk_, :].rearrange("p (h c) -> p h c", h=H)
                    dve.wait_ge(un_ok, t * TT + a + 1)
                    dve.reciprocal(rden[:, a, :], u[:, :, DH:DH + 1].rearrange("p h o -> p (h o)")).then_inc(rd_ok, 1)
                    dve.wait_ge(rd_ok, t * TT + a + 1)
                    if a == 0 and (not isinstance(i, int) or t >= 1):
                        dve.wait_ge(at_ok, t)
                    dve.tensor_tensor(att[:, a, :].rearrange("p (h d) -> p h d", h=H), u[:, :, 0:DH],
                                      rden[:, a, :].rearrange("p (h o) -> p h o", o=1).broadcast_to([P, H, DH]),
                                      op=ALU.mult).then_inc(att_ok, 1)

                def second_apply():
                    if not gates:
                        return
                    gt = i - 2
                    if not isinstance(i, int) or gt >= 1:
                        dve.wait_ge(xt2_ok, gt)
                    norm_apply(X[:, tiles(gt), :], xn2, gt, mv2, rstd2, rs2, xn2_ok)

                def residual():
                    t = i - 1
                    dve.wait_ge(wo_ok, t + 1)
                    dve.wait_ge(bo_ok, t + 1)
                    dve.tensor_tensor(X[:, tiles(t), :], ps[:, PM, 0:S].rearrange("p (a d) -> p a d", a=TT),
                                      X[:, tiles(t), :], op=ALU.add).then_inc(x2_ok, 1)

                def split_maxima():
                    a = i + 1
                    if tail:
                        dve.wait_ge(x2_ok, i)
                    if maxima:
                        dve.wait_ge(mx_ok, a * H + H)
                        if not isinstance(i, int) or a >= 1:
                            dve.wait_ge(mt_ok, a)
                        m = MX[:, :, :].rearrange("p a (g j) -> p a g j", g=G)
                        dve.tensor_scalar(MHL[:, :, :, 0, :], m, -1.0, None, ALU.mult).then_inc(mh_ok, 1)
                        dve.wait_ge(mh_ok, a + 1)
                        for qt in range(TT):
                            last = dve.scalar_tensor_tensor(
                                MHL[:, qt, :, 1, :], m[:, qt, :, :], -1.0, MHL[:, qt, :, 0, :].bitcast(F32),
                                op0=ALU.mult, op1=ALU.subtract)
                        last.then_inc(ml_ok, 1)

                reduce(0)
                if gates:
                    dve.wait_ge(st2, i - 1)
                if scores:
                    dve.wait_ge(mt_ok, i + 1)
                    if not isinstance(i, int) or i >= 1:
                        for g in range(G):
                            dve.wait_ge(sh_ok[g], 16 * i)
                    dve.tensor_copy(MT[:, :], ps[0:32, PM, 0:S]).then_inc(mts_ok, 1)
                if gates:
                    norm_mean(i - 2, stat2, mv2, veps2, mvs2, ve2)
                reduce(1)
                reduce(2)
                second_apply()
                reduce(3)
                if front:
                    rope_mul(0, q_ok, 0, rq_ok)
                reduce(4)
                if front:
                    rope_mul(1, k_ok, 1, rk_ok)
                if front:
                    values()
                reduce(5)
                if more:
                    if isinstance(i, int) and i < 0:
                        for n in ((1,) if i == -2 else (2, 3)):
                            dve.wait_ge(xld[n], 16)
                    norm_stats(X[:, tiles(i + 3), :], stat, st1)
                    dve.wait_ge(st1, i + 4)
                reduce(6)
                if more:
                    norm_mean(i + 3, stat, mv, veps, mv1, ve1)
                reduce(7)
                reduce(8)
                if tail:
                    normalise(0)
                reduce(9)
                if tail:
                    normalise(1)
                reduce(10)
                reduce(11)
                if more:
                    first_apply(i + 3, False)
                reduce(12); reduce(13)
                if tail:
                    residual()
                reduce(14); reduce(15)
                split_maxima()
                if tail:
                    norm_stats(X[:, tiles(i - 1), :], stat2, st2)

            run(dve, iteration)

            steps = [0]

            def step(ins):
                steps[0] += 1
                ins.then_inc(rt, 1)
                dve.wait_ge(rt, steps[0])

            dve.wait_ge(sb_ok, NB * H)
            dve.wait_ge(kz_ok, NB * G)
            dve.tensor_tensor(SEL, ident[0:2 * NE, 0:NE].rearrange("p (e o) -> p e o", o=1)
                              .broadcast_to([2 * NE, NE, P]),
                              ident[0:2 * NE, NE:2 * NE].rearrange("p (e o) -> p e o", o=1)
                              .broadcast_to([2 * NE, NE, P]), op=ALU.add).then_inc(sel_ok, 1)
            dve.wait_ge(pv_ok, NB * G)
            dve.wait_ge(ge_ok, NB)
            step(dve.tensor_scalar(gate, GE[:, :, :], 1.0, None, ALU.add))
            step(dve.reciprocal(gate, gate))
            dve.memset(vx_flat[:, 4 * NT * NE:12 * NT * NE].rearrange("p (t k) -> p t k", t=NT)[:, :, 0:NE * NE:NE + 1],
                       0.0)
            for j in range(NE):
                for e0, e1, op in ((0, j, ALU.is_gt), (j + 1, NE, ALU.is_ge)):
                    if e0 < e1:
                        last = dve.tensor_tensor(beats[:, :, e0:e1, j], gate[:, :, j:j + 1].broadcast_to([P, NT, e1 - e0]),
                                                 gate[:, :, e0:e1], op=op)
            step(last)
            step(dve.tensor_reduce(rank, beats, op=ALU.add, axis=AX.X))
            step(dve.scalar_tensor_tensor(wsel, rank, 2.0, gate, op0=ALU.is_lt, op1=ALU.mult))
            step(dve.tensor_reduce(wsum, wsel, op=ALU.add, axis=AX.X))
            step(dve.reciprocal(wrec, wsum))
            step(dve.scalar_tensor_tensor(wpart, wsel, 1.0 / 3.0, wrec.broadcast_to([P, NT, NE]),
                                          op0=ALU.mult, op1=ALU.mult))
            step(dve.tensor_copy(WHL[:, :, 0, :], wpart))
            step(dve.tensor_tensor(WHL[:, :, 1, :], wpart, WHL[:, :, 0, :].bitcast(F32), op=ALU.subtract))

            def hidden_lo(n, q):
                dve.wait_ge(hh_ok, n + 1)
                dve.tensor_tensor(hid_part[:, q % 3, 1, :], hid[:, q % 2, :], hid_part[:, q % 3, 0, :].bitcast(F32),
                                  op=ALU.subtract).then_inc(hl_ok, 1)

            def residual(c):
                dve.wait_ge(y_t, c + 1)
                rows = X[:, bass.ds(c * CT, CT), :]
                dve.tensor_tensor(rows, ps[:, M0 + 1, :].rearrange("p (a d) -> p a d", a=CT), rows,
                                  op=ALU.add).then_inc(y_ok, 1)

            def chunk(c):
                dyn = not isinstance(c, int)
                if dyn or c >= 1:
                    dve.wait_ge(wt_t, c)
                dve.tensor_copy(WC[:, :, :], WHL[:, bass.ds(c * CT, CT), :, :].rearrange("p t l e -> p t (l e)")
                                .bitcast(F32)).then_inc(wc_ok, 1)
                for q in range(HV):
                    n = c * HV + q
                    if dyn or n >= 1:
                        hidden_lo(n - 1, (q - 1) % HV)
                    if q < FH:
                        dve.wait_ge(si_ok, n + 1)
                        dve.scalar_tensor_tensor(hid[:, q % 2, :], silu[:, q % 2, :], 1.0 / 3.0, ps[:, U0 + q % 2, :],
                                                 op0=ALU.mult, op1=ALU.mult).then_inc(h_ok, 1)
                    else:
                        dve.wait_ge(sw_ok, c * NE * FH + q - FH + 1)
                        dve.tensor_tensor(hid[:, q % 2, :], silw[:, q % 2, :], ps[:, U0 + q % 2, :],
                                          op=ALU.mult).then_inc(h_ok, 1)
                    if q == 0:
                        if dyn or c >= 1:
                            dve.wait_ge(wb_t, c * NE)
                        dve.wait_ge(wt_t, c + 1)
                        dve.tensor_copy(WT, ps[0:2 * NE, M0, :]).then_inc(wt_ok, 1)
                    if q == 5 and (dyn or c >= 1):
                        residual(c - 1)

            chunk(0)
            with dve.Fori(1, NCH, 1) as c:
                chunk(c)
            hidden_lo(NCH * HV - 1, HV - 1)
            residual(NCH - 1)

        @block.tensor
        def _(pe):
            mm = pe.matmul
            pe.wait_ge(ld, 16 * NLD)
            pe.wait_ge(setup_pool, 2)

            def heads_out(b, pb, g):
                dyn = not isinstance(b, int)
                pe.wait_ge(ex_ok, b * H + 4 * g + 4)
                if g == 0:
                    pe.wait_ge(vx_ok, b + 1)
                    if dyn or b >= 1:
                        pe.wait_ge(ut_ok, b * 2)
                if g == 2:
                    pe.wait_ge(ut_ok, b * 2 + 1)
                for kt in range(TT):
                    for j in range(J):
                        last = mm(ps[32 * j:32 * j + 32, PU, (g % 2) * S:(g % 2 + 1) * S],
                                  VX[:, pb, kt, G * g + j, :], PR[:, (G * g + j) % 8, kt, :],
                                  start=kt == 0, stop=kt == TT - 1)
                last.then_inc(pv_ok, 1)

            def iteration(i, ph, has, _):
                front, maxima, scores, tail, gates = has
                dyn = not isinstance(i, int)
                f, t, gt = i + 2, i - 1, i - 2
                pa = (ph + 1) % NBUF

                def unit(u):
                    if not maxima:
                        return
                    a = i + 1
                    if u % G == 0:
                        pe.wait_ge(kz_ok, a * G + u // G + 1)
                    n = a * H + u
                    if dyn or n >= 2:
                        pe.wait_ge(mx_ok, n - 1)
                    hp, qt = u // 2, u % 2
                    g, j = hp // 2, 2 * (hp % 2)
                    mm(ps[:, SA + u % 2, :], QK[0:KA, pa, 0, g, qt * P:(qt + 1) * P],
                       KZ[0:KA, pa, g, j:j + 2, :], start=True, stop=True).then_inc(sa_ok, 1)

                def head(h):
                    if not scores:
                        return
                    n = i * H + h
                    if h % J == 0:
                        pe.wait_ge(sh_ok[h // J], (i + 1) * 16)
                    if dyn or n >= 3:
                        pe.wait_ge(ex_ok, n - 2)
                    g, j = h // J, h % J
                    for kt in range(TT):
                        last = mm(ps[:, SB + (ph + h) % 3, kt * S:(kt + 1) * S],
                                  KZ[0:KB, ph, g, j, kt * P:(kt + 1) * P], QK[0:KB, ph, 0, g, :],
                                  start=True, stop=True)
                    last.then_inc(sb_ok, 1)

                def project(n, bank_, done):
                    for s, w in enumerate((wraw[:, 2 * n, :], wraw[:, 2 * n + 1, :])):
                        last = mm(ps[:, PM + bank_, s * S:(s + 1) * S], w, xnT[:, :], start=True, stop=True)
                    last.then_inc(done, 1)

                def back_to_rows(a, bank_):
                    for g in range(G):
                        last = pe.transpose(ps[:, PM + bank_, g * P:(g + 1) * P], UT[:, g, a * P:(a + 1) * P], ident)
                    last.then_inc(un_ok, 1)

                def maxima_rows():
                    if not scores:
                        return
                    pe.wait_ge(ml_ok, i + 1)
                    if dyn or i >= 2:
                        pe.wait_ge(x2_ok, i - 1)
                    else:
                        pe.wait_ge(vx_ok, i + 2)
                    for a in range(TT):
                        last = pe.transpose(ps[0:32, PM, a * P:(a + 1) * P],
                                            MHL[:, a, :, :, :].rearrange("p g l j -> p (g l j)").bitcast(F32), ident)
                    last.then_inc(mt_ok, 1)

                def front_tokens():
                    if not front:
                        return
                    pe.wait_ge(xn_ok, f + 1)
                    if dyn or i >= 2:
                        pe.wait_ge(atT_ok, i - 1)
                    elif i >= -1:
                        pe.wait_ge(rk_ok, f)
                    for a in range(TT):
                        last = pe.transpose(ps[:, PM + 1, a * P:(a + 1) * P], xn[:, a, :], ident)
                    last.then_inc(xt_ok, 1)

                def queries():
                    if not front:
                        return
                    pe.wait_ge(xnT_ok, f + 1)
                    if scores:
                        pe.wait_ge(mts_ok, i + 1)
                    elif i == -1:
                        pe.wait_ge(vx_ok, f)
                    project(0, 0, q_ok)

                def keys():
                    if front:
                        project(1, 1, k_ok)

                def values():
                    if not front:
                        return
                    pe.wait_ge(rq_ok, f + 1)
                    for a in range(TT):
                        last = mm(ps[:, PM, a * P:(a + 1) * P], xnT[:, a * P:(a + 1) * P], wraw[:, 4, :],
                                  start=True, stop=True)
                    last.then_inc(v_ok, 1)

                def second_tokens():
                    if not gates:
                        return
                    pe.wait_ge(xn2_ok, gt + 1)
                    if front:
                        pe.wait_ge(rk_ok, f + 1)
                    else:
                        pe.wait_ge(atT_ok, i - 1)
                    for a in range(TT):
                        last = pe.transpose(ps[:, PM + 1, a * P:(a + 1) * P], xn2[:, a, :], ident)
                    last.then_inc(xt2_ok, 1)

                def gate_logits():
                    if not gates:
                        return
                    pe.wait_ge(xf_ok, gt + 1)
                    if front:
                        pe.wait_ge(vx_ok, f + 1)
                    elif scores:
                        pe.wait_ge(mts_ok, i + 1)
                    else:
                        pe.wait_ge(x2_ok, i - 1)
                    for a in range(TT):
                        last = mm(ps[:, PM, a * NE:(a + 1) * NE], xf[:, a * P:(a + 1) * P], wg[:, :],
                                  start=True, stop=True)
                    last.then_inc(g_ok, 1)

                def rows_0():
                    if not tail:
                        return
                    pe.wait_ge(ut_ok, t * 2 + 2)
                    if gates:
                        pe.wait_ge(xf_ok, gt + 1)
                    elif front:
                        pe.wait_ge(rk_ok, f + 1)
                    back_to_rows(0, 1)

                def rows_1():
                    if not tail:
                        return
                    if gates:
                        pe.wait_ge(ge_ok, gt + 1)
                    elif front:
                        pe.wait_ge(vx_ok, f + 1)
                    back_to_rows(1, 0)

                def attention_T():
                    if not tail:
                        return
                    pe.wait_ge(att_ok, t * TT + TT)
                    for a in range(TT):
                        last = pe.transpose(ps[:, PM + 1, a * P:(a + 1) * P], att[:, a, :], ident)
                    last.then_inc(at_ok, 1)

                def output():
                    if not tail:
                        return
                    pe.wait_ge(atT_ok, t + 1)
                    for a in range(TT):
                        last = mm(ps[:, PM, a * P:(a + 1) * P], attT[:, a * P:(a + 1) * P], wraw[:, 5, :],
                                  start=True, stop=True)
                    last.then_inc(wo_ok, 1)

                def heads(g):
                    if scores:
                        heads_out(i, ph, g)

                unit(0); front_tokens(); unit(1)
                maxima_rows()
                if tail:
                    heads_out(t, (ph - 1) % NBUF, 3)
                unit(2); queries()
                unit(3); keys()
                unit(4); head(0); head(1); values()
                unit(5); head(2); head(3)
                unit(6); second_tokens(); head(4)
                unit(7); head(5); head(6)
                unit(8); heads(0); head(7); rows_0()
                unit(9); gate_logits(); head(8); head(9); rows_1()
                unit(10); head(10); heads(1)
                unit(11); head(11); attention_T()
                unit(12); head(12); output()
                unit(13); head(13); heads(2)
                unit(14); head(14)
                unit(15); head(15)

            run(pe, iteration)

            pe.wait_ge(sel_ok, 1)
            pe.wait_ge(xl_ok, NB)
            pe.wait_ge(ge_ok, NB)
            pe.wait_ge(ut_ok, NB * 2)

            def up(c, q):
                dyn = not isinstance(c, int)
                n = c * HV + q
                e, v = q // FH, q % FH
                if not dyn and c == 0:
                    pe.wait_ge(wl_ok, e + 1)
                if dyn or n >= 2:
                    pe.wait_ge(h_ok, n - 1)
                tok = bass.ds(c * CH, CH)
                for b, w in ((G0, v * P), (U0, F + v * P)):
                    for k, (l, part) in enumerate(((0, XH), (0, XL), (1, XH))):
                        last = mm(ps[:, b + q % 2, :], w_up_part[l][:, e, w:w + P], part[:, tok],
                                  start=k == 0, stop=k == 2)
                last.then_inc(gu_ok, 1)

            def down(c, q):
                e, v = q // FH, q % FH
                if q == 0 and (not isinstance(c, int) or c >= 1):
                    pe.wait_ge(yT_ok, c)
                pe.wait_ge(hl_ok, c * HV + q + 1)
                for k, (l, m) in enumerate(((0, 0), (0, 1), (1, 0))):
                    last = mm(ps[:, Y0, :], w_dn_part[l][:, e, v, :], hid_part[:, q % 3, m, :],
                              start=q == 0 and k == 0, stop=q == HV - 1 and k == 2)
                last.then_inc(dn_ok, 1)

            def sum_rows(c):
                pe.wait_ge(yT_ok, c + 1)
                for a in range(CT):
                    last = pe.transpose(ps[:, M0 + 1, a * P:(a + 1) * P], yT[:, a * P:(a + 1) * P], ident)
                last.then_inc(y_t, 1)

            def chunk(c):
                dyn = not isinstance(c, int)
                for k in range(NEX):
                    for q in (2 * k, 2 * k + 1):
                        up(c, q)
                        if q >= 2:
                            down(c, q - 2)
                        elif dyn or c >= 1:
                            down(c - 1, HV - 2 + q)
                        if q == 0:
                            if dyn or c >= 1:
                                pe.wait_ge(wb_ok, c * NE - 1)
                            pe.wait_ge(wc_ok, c + 1)
                            for a in range(CT):
                                last = pe.transpose(ps[0:2 * NE, M0, a * P:(a + 1) * P], WC[:, a, :], ident)
                            last.then_inc(wt_t, 1)
                    e = k + 1
                    if e <= NE:
                        if e == 1:
                            pe.wait_ge(wt_ok, c + 1)
                            if dyn or c >= 1:
                                pe.wait_ge(wb_ok, c * NE)
                        elif e == 3:
                            pe.wait_ge(wb_ok, c * NE + 2)
                        elif e == 4 and (dyn or c >= 1):
                            pe.wait_ge(y_ok, c)
                        elif e >= 4:
                            pe.wait_ge(wb_ok, c * NE + e - 2)
                        mm(ps[:, wrow_bank(e), :], SEL[:, e - 1, :], WT, start=True, stop=True).then_inc(wb_t, 1)
                    if k == 1 and (dyn or c >= 1):
                        pe.wait_ge(wb_ok, c * NE + 1)
                        sum_rows(c - 1)

            chunk(0)
            with pe.Fori(1, NCH, 1) as c:
                chunk(c)
            for q in (HV - 2, HV - 1):
                down(NCH - 1, q)
            sum_rows(NCH - 1)


def constants():
    import numpy as np
    c = np.zeros((P, C_ALL), np.float32)
    inv_freq = (1.0 / 10000.0 ** (np.arange(0, DH, 2, dtype=np.float32) / np.float32(DH))).astype(np.float32)
    freqs = np.arange(S, dtype=np.float32)[:, None] * inv_freq[None, :]
    ang = np.concatenate((freqs, freqs), axis=-1)[:, ::2].astype(np.float32)
    for p in range(P):
        a = ang[:, (p % DH) // 2]
        c[p, C_ROPE:C_ROPE + S] = np.cos(a)
        c[p, C_ROPE + S:C_ROPE + 2 * S] = np.sin(a) if p % 2 else -np.sin(a)
        c[p, C_IDENT + p] = 1.0
        if p < KA:
            c[p, C_MASK + p % 32 // DH] = 1.0
        elif p < KB:
            c[p, C_MASK + p % J] = 1.0
    return c


def kernel(L0_attn_x, L0_attn_Wq, L0_attn_bq, L0_attn_Wk, L0_attn_bk, L0_attn_Wv, L0_attn_bv, L0_attn_Wo, L0_attn_bo,
           L0_ffn_Wg, L0_ffn_Ws1, L0_ffn_Ws3, L0_ffn_Ws2, L0_ffn_We1, L0_ffn_We3, L0_ffn_We2):
    import numpy as np
    import concourse.bacc as bacc
    from concourse.bass_utils import run_bass_kernel_spmd

    def swapped(a):
        a = np.asarray(a)
        return a.reshape(a.shape[:-1] + (a.shape[-1] // 2, 2))[..., ::-1].reshape(a.shape)

    w_att = np.concatenate([np.asarray(L0_attn_Wq), swapped(L0_attn_Wq), np.asarray(L0_attn_Wk),
                            swapped(L0_attn_Wk), np.asarray(L0_attn_Wv), np.asarray(L0_attn_Wo)], axis=1)
    b_cols = np.stack([np.asarray(L0_attn_bq), swapped(L0_attn_bq), np.asarray(L0_attn_bk), swapped(L0_attn_bk)], axis=1)
    w1 = np.concatenate([np.asarray(L0_ffn_Ws1)[None], np.asarray(L0_ffn_We1)])
    w3 = np.concatenate([np.asarray(L0_ffn_Ws3)[None], np.asarray(L0_ffn_We3)])
    w2 = np.concatenate([np.asarray(L0_ffn_Ws2)[None], np.asarray(L0_ffn_We2)])
    w_up = np.concatenate([w1, w3], axis=2).transpose(1, 0, 2)
    w_down = w2.reshape(NEX, FH, P, D).transpose(2, 0, 1, 3)

    nc = bacc.Bacc("TRN2", target_bir_lowering=False, num_devices=1)
    arrays, args = {}, []
    for name, a in (("x", L0_attn_x), ("w_att", w_att), ("b_cols", b_cols), ("bv", L0_attn_bv), ("bo", L0_attn_bo),
                    ("Wg", L0_ffn_Wg), ("w_up", w_up), ("w_down", w_down), ("const", constants())):
        a = np.ascontiguousarray(a)
        arrays[f"in_{name}"] = a
        args.append(nc.dram_tensor(f"in_{name}", a.shape, mybir.dt.from_np(a.dtype), kind="ExternalInput").ap())
    args.append(nc.dram_tensor("out_0", (NB, S, D), F32, kind="ExternalOutput").ap())
    layer_kernel(nc, *args)
    r = run_bass_kernel_spmd(nc, [arrays], core_ids=[0])
    return r.results[0]["out_0"]
```

```python
from contextlib import ExitStack

import concourse.bass as bass
from concourse import mybir

ALU = mybir.AluOpType
ACT = mybir.ActivationFunctionType
AX = mybir.AxisListType
F32 = mybir.dt.float32
F32R = mybir.dt.float32r

P = 128
NB = 16
S = 256
D = 128
H = 16
DH = 8
G = 4
J = 4
TT = S // P
NT = NB * TT
F = 256
FH = F // P
NE = 8
NEX = NE + 1
CH = 512
NCH = NB * S // CH
CT = CH // P
KA = 96
KB = 104
NBUF = 3
SCALE = float(DH) ** -0.5
EPS = 1e-5

C_ROPE = 0
C_IDENT = C_ROPE + 2 * S
C_MASK = C_IDENT + P
C_ALL = C_MASK + J


def layer_kernel(nc, x, w_att, b_cols, bv, bo, Wg, w_up, w_down, const, out):
    with ExitStack() as ctx:
        def sb(name, shape, dt=F32):
            return ctx.enter_context(nc.sbuf_tensor(name, shape, dt))

        def sem(name):
            return ctx.enter_context(nc.semaphore(name))

        X = sb("X", [P, NT, D])
        cst = sb("cst", [P, C_ALL])
        wraw = sb("wraw", [P, 6, D])
        wg = sb("wg", [P, NE])
        bcol = sb("bcol", [P, 4])
        brow = sb("brow", [P, 2, D])
        stat = sb("stat", [P, TT, 6])
        mv = sb("mv", [P, TT, 2])
        veps = sb("veps", [P, TT])
        rstd = sb("rstd", [P, TT])
        halves = sb("halves", [P, TT])
        stat2 = sb("stat2", [P, TT, 6])
        mv2 = sb("mv2", [P, TT, 2])
        veps2 = sb("veps2", [P, TT])
        rstd2 = sb("rstd2", [P, TT])
        xn = sb("xn", [P, TT, D])
        xn2 = sb("xn2", [P, TT, D])
        xnT = sb("xnT", [P, S])
        rc = sb("rc", [P, 2, S])
        rs = sb("rs", [P, 2, S])
        HL = sb("HL", [P, 2, 2, S], F32R)
        QK = sb("QK", [P, NBUF, 2, G, S], F32R)
        KZ = sb("KZ", [P, NBUF, G, J, S], F32R)
        VX = sb("VX", [P, NBUF, TT, H, 32])
        MX = sb("MX", [P, TT, H])
        MHL = sb("MHL", [P, TT, G, 2, J], F32R)
        MT = sb("MT", [32, S], F32R)
        PR = sb("PR", [P, 8, TT, S])
        UT = sb("UT", [P, G, S])
        rden = sb("rden", [P, TT, H])
        att = sb("att", [P, TT, D])
        attT = sb("attT", [P, S])
        xf = sb("xf", [P, S])
        XH = sb("XH", [P, NB * S], F32R)
        XL = sb("XL", [P, NB * S], F32R)
        GE = sb("GE", [P, NT, NE])
        WHL = sb("WHL", [P, NT, 2, NE], F32R)
        WC = sb("WC", [P, CT, 2 * NE])
        up_raw = sb("up_raw", [P, NEX, 2 * F])
        dn_raw = sb("dn_raw", [P, NEX, FH, D])
        kz_flat = KZ[:, :, :, :, :].rearrange("p n g j t -> p (n g j t)")
        qk_flat = QK[:, :, :, :, :].rearrange("p n a g t -> p (n a g t)")
        UPW, DNW = 2 * 2 * F, 2 * FH * D
        HIDW = 3 * 2 * CH
        KZ1, QK1 = G * J * S, 2 * G * S

        def up_part(e, l):
            at = KZ1 + e * UPW if e < NE else HIDW
            return kz_flat[:, at + l * 2 * F:at + (l + 1) * 2 * F]

        def dn_part(e, l):
            at = QK1 + e * DNW if e < NE else NE * P + CH
            return qk_flat[:, at + l * FH * D:at + (l + 1) * FH * D].rearrange("p (v d) -> p v d", v=FH)

        hid_part = kz_flat[:, 0:HIDW].rearrange("p (n l t) -> p n l t", n=3, l=2)
        SEL = qk_flat[0:2 * NE, 0:NE * P].rearrange("p (e m) -> p e m", e=NE)
        WT = qk_flat[0:2 * NE, NE * P:NE * P + CH]
        work = PR[:, :, :, :].rearrange("p n a t -> p n (a t)")
        silu, silw, hid, wrow = work[:, 0:2, :], work[:, 2:4, :], work[:, 4:6, :], work[:, 6:8, :]
        yT = UT[:, :, :].rearrange("p g t -> p (g t)")[:, 0:CH]
        vx_flat = VX[:, :, :, :, :].rearrange("p n a h c -> p (n a h c)")

        def routing_tiles(n):
            at = TT * H * 32
            four = [vx_flat[:, at + k * n * NE:at + (k + 1) * n * NE].rearrange("p (t e) -> p t e", t=n)
                    for k in range(4)]
            flat = vx_flat[:, at + 4 * n * NE:at + (4 + NE) * n * NE]
            return four + [flat.rearrange("p (t e j) -> p t e j", t=n, e=NE),
                           flat.rearrange("p (t k) -> p t k", t=n)]

        ps = ctx.enter_context(nc.psum_tensor("ps", [P, 8, 512], F32))
        SA, SB, PU, PM = 0, 2, 5, 6

        cst_ld = sem("cst_ld")
        wqk_ld = sem("wqk_ld")
        bcol_ld = sem("bcol_ld")
        ld = sem("ld")
        wld = sem("wld")
        xld = [sem(f"xld{n}") for n in range(4)]
        setup_dve = sem("setup_dve")
        setup_pool = sem("setup_pool")
        ve1 = sem("ve1"); ve2 = sem("ve2"); st1 = sem("st1"); mv1 = sem("mv1"); rs1 = sem("rs1")
        st2 = sem("st2"); mvs2 = sem("mvs2"); rs2 = sem("rs2")
        xn_ok = sem("xn_ok")
        xn2_ok = sem("xn2_ok")
        xt_ok = sem("xt_ok")
        xnT_ok = sem("xnT_ok")
        q_ok = sem("q_ok"); k_ok = sem("k_ok"); v_ok = sem("v_ok")
        rq_ok = sem("rq_ok"); rk_ok = sem("rk_ok")
        vx_ok = sem("vx_ok")
        bo_ok = sem("bo_ok")
        rot_ok = sem("rot_ok"); hi_ok = sem("hi_ok"); lo_ok = sem("lo_ok")
        qk_ok = [sem(f"qk_ok{g}") for g in range(G)]
        kz_ok = sem("kz_ok")
        sa_ok = sem("sa_ok")
        mx_ok = sem("mx_ok")
        mh_ok = sem("mh_ok"); ml_ok = sem("ml_ok")
        mt_ok = sem("mt_ok")
        mts_ok = sem("mts_ok")
        sh_ok = [sem(f"sh_ok{g}") for g in range(G)]
        sb_ok = sem("sb_ok")
        ex_ok = sem("ex_ok")
        pv_ok = sem("pv_ok")
        ut_ok = sem("ut_ok")
        un_ok = sem("un_ok")
        rd_ok = sem("rd_ok")
        att_ok = sem("att_ok")
        at_ok = sem("at_ok")
        atT_ok = sem("atT_ok")
        wo_ok = sem("wo_ok")
        x2_ok = sem("x2_ok")
        xt2_ok = sem("xt2_ok"); xf_ok = sem("xf_ok"); xh_ok = sem("xh_ok"); xl_ok = sem("xl_ok")
        g_ok = sem("g_ok")
        ge_ok = sem("ge_ok")

        wh_ok = sem("wh_ok"); wl_ok = sem("wl_ok")
        sel_ok = sem("sel_ok")
        rt = sem("rt")
        wc_ok = sem("wc_ok"); wt_t = sem("wt_t"); wt_ok = sem("wt_ok")
        wb_t = sem("wb_t"); wb_ok = sem("wb_ok")
        gu_ok = sem("gu_ok")
        si_ok = sem("si_ok")
        sw_ok = sem("sw_ok")
        h_ok = sem("h_ok"); hh_ok = sem("hh_ok"); hl_ok = sem("hl_ok")
        dn_ok = sem("dn_ok")
        yT_ok = sem("yT_ok"); y_t = sem("y_t"); y_ok = sem("y_ok")
        out_ok = sem("out_ok")

        HV = NEX * FH
        G0, U0, Y0, M0 = 0, 2, 4, 5

        rope = cst[:, C_ROPE:C_ROPE + 2 * S].rearrange("p (a t) -> p a t", a=2)
        ident = cst[:, C_IDENT:C_IDENT + P]

        def mask(j):
            return cst[:, C_MASK + j:C_MASK + j + 1]

        x_v = x.rearrange("b (a p) d -> p (b a) d", p=P)
        out_v = out.rearrange("b (a p) d -> p (b a) d", p=P)
        XLOADS = (0, 2, 4, 16, NT)
        NLD = 4
        STACKS = 3

        def wrow_bank(e):
            return M0 + (e % 2 if e < 3 else (e + 1) % 2)

        def tiles(b):
            return bass.ds(b * TT, TT)

        def stages(i):
            return (0 <= i + 2 < NB, 0 <= i + 1 < NB, 0 <= i < NB, 0 <= i - 1 < NB, 0 <= i - 2 < NB)

        def run(eng, iteration):
            first = NBUF
            turns = (NB - 3 - first) // NBUF
            for i in range(-2, first):
                iteration(i, i % NBUF, stages(i), i)
            with eng.Fori(first, first + (turns - 1) * NBUF + 1, NBUF) as base:
                for r in range(NBUF):
                    iteration(base + r, (first + r) % NBUF, (True,) * 5, first)
            for i in range(first + turns * NBUF, NB + 2):
                iteration(i, i % NBUF, stages(i), i)

        block = ctx.enter_context(nc.Block())

        @block.sync
        def _(sp):
            for n, (lo, hi) in enumerate(zip(XLOADS, XLOADS[1:])):
                sp.dma_start(X[:, lo:hi, :], x_v[:, lo:hi, :]).then_inc(xld[n], 16)
                if n == 0:
                    sp.dma_start(cst[:, :], const).then_inc(cst_ld, 16)
                    sp.dma_start(wraw[:, 0:4, :], w_att[:, 0:4 * D].rearrange("p (n d) -> p n d", n=4)).then_inc(wqk_ld, 16)
                    sp.dma_start(bcol[:, :], b_cols).then_inc(bcol_ld, 16)
                    sp.dma_start(wraw[:, 4:6, :], w_att[:, 4 * D:6 * D].rearrange("p (n d) -> p n d", n=2)).then_inc(ld, 16)
            sp.dma_start(wg[:, :], Wg).then_inc(ld, 16)
            for n, b in enumerate((bv, bo)):
                sp.dma_start(brow[:, n, :], b.rearrange("(o d) -> o d", o=1).broadcast_to([P, D])).then_inc(ld, 16)

            sp.dma_start(up_raw[:, :, :], w_up).then_inc(wld, 16)
            sp.dma_start(dn_raw[:, :, :, :], w_down).then_inc(wld, 16)

            def iteration(i, ph, has, _):
                front, _, scores, _, _ = has
                if scores:
                    sp.wait_ge(mts_ok, i + 1)
                    for g in range(G):
                        sp.dma_start(QK[KA:KB, ph, 0, g, :].bitcast(F32), MT[8 * g:8 * g + 8, :].bitcast(F32)).then_inc(sh_ok[g], 16)
                if front:
                    f, pf = i + 2, (ph + 2) % NBUF
                    sp.wait_ge(lo_ok, f + 1)
                    flat = HL[:, :, :, :].rearrange("p a b t -> p (a b) t")
                    for g in range(G):
                        for r, (q, k) in enumerate(((0, 2), (1, 2), (0, 3))):
                            sp.dma_start(QK[32 * r:32 * r + 32, pf, :, g, :].bitcast(F32),
                                         flat[32 * g:32 * g + 32, q:k + 1:k - q, :].bitcast(F32)).then_inc(qk_ok[g], 16)

            run(sp, iteration)

            def store(c):
                sp.wait_ge(y_ok, c + 1)
                sp.dma_start(out_v[:, bass.ds(c * CT, CT), :], X[:, bass.ds(c * CT, CT), :]).then_inc(out_ok, 16)

            with sp.Fori(0, NCH, 1) as c:
                store(c)
            sp.wait_ge(out_ok, 16 * NCH)

        @block.gpsimd
        def _(pool):
            pool.memset(VX[:, :, :, :, :], 0.0).then_inc(setup_pool, 1)
            pool.wait_ge(setup_pool, 1)
            pool.memset(VX[:, :, :, :, DH:DH + 1], 1.0).then_inc(setup_pool, 1)
            pool.wait_ge(setup_dve, NBUF + 1)

            def root(b, v, r, ready, done):
                pool.wait_ge(ready, b + 1)
                pool.tensor_tensor(r[:, :], v[:, :], halves[:, :], op=ALU.pow).then_inc(done, 1)

            root(0, veps, rstd, ve1, rs1)
            pool.wait_ge(cst_ld, 16)
            pool.wait_ge(ld, 16 * NLD)

            def split_weights(e):
                pool.tensor_scalar(up_part(e, 0), up_raw[:, e, :], 1.0, 1.0, ALU.mult, ALU.mult)
                pool.tensor_scalar(dn_part(e, 0), dn_raw[:, e, :, :], 1.0, 1.0, ALU.mult, ALU.mult).then_inc(wh_ok, 1)
                pool.wait_ge(wh_ok, e + 1)
                pool.tensor_tensor(up_part(e, 1), up_raw[:, e, :], up_part(e, 0).bitcast(F32), op=ALU.subtract)
                pool.tensor_tensor(dn_part(e, 1), dn_raw[:, e, :, :], dn_part(e, 0).bitcast(F32),
                                   op=ALU.subtract).then_inc(wl_ok, 1)

            def iteration(i, ph, has, _):
                front, _, _, _, gates = has
                if front:
                    f, pf = i + 2, (ph + 2) % NBUF
                    pool.wait_ge(xn_ok, f + 1)
                    pool.tensor_tensor(X[:, tiles(f), :], X[:, tiles(f), :],
                                       brow[:, 1:2, :].broadcast_to([P, TT, D]), op=ALU.add).then_inc(bo_ok, 1)
                    pool.wait_ge(rk_ok, f + 1)
                    pool.wait_ge(rq_ok, f + 1)
                    pool.tensor_tensor(rc[:, :, :], rc[:, :, :], rs[:, :, :], op=ALU.add).then_inc(rot_ok, 1)
                    pool.wait_ge(hi_ok, f + 1)
                    pool.tensor_tensor(HL[:, :, 1, :], rc[:, :, :], HL[:, :, 0, :].bitcast(F32),
                                       op=ALU.subtract).then_inc(lo_ok, 1)
                if front and (not isinstance(i, int) or i + 3 < NB):
                    root(i + 3, veps, rstd, ve1, rs1)
                if gates:
                    root(i - 2, veps2, rstd2, ve2, rs2)
                if isinstance(i, int) and NB - 2 <= i <= NB:
                    pool.wait_ge(sb_ok, i * H)
                    if i == NB - 2:
                        pool.wait_ge(wld, 32)
                    per = NE // 2
                    for e in range((i - NB + 2) * per, min((i - NB + 3) * per, NEX)):
                        split_weights(e)
                if front:
                    for g in range(G):
                        pool.wait_ge(qk_ok[g], 16 * STACKS * (f + 1))
                        pool.tensor_tensor(KZ[:, pf, g, 0, :], QK[:, pf, 1, g, :].bitcast(F32),
                                           mask(0).broadcast_to([P, S]), op=ALU.mult)
                        for j in range(1, J):
                            last = pool.tensor_scalar(KZ[:, pf, g, j, :], QK[:, pf, 1, g, :].bitcast(F32),
                                                      mask(j), 1.0, ALU.mult, ALU.mult)
                        last.then_inc(kz_ok, 1)
                if gates:
                    t = i - 2
                    pool.wait_ge(xh_ok, t + 1)
                    tok = bass.ds(t * S, S)
                    pool.tensor_tensor(XL[:, tok], xf[:, :], XH[:, tok].bitcast(F32),
                                       op=ALU.subtract).then_inc(xl_ok, 1)

            run(pool, iteration)

            def chunk(c):
                for q in range(FH, HV):
                    e = q // FH
                    pool.wait_ge(h_ok, c * HV + q - 1)
                    pool.wait_ge(wb_ok, c * NE + e)
                    pool.wait_ge(si_ok, c * HV + q + 1)
                    pool.tensor_tensor(silw[:, q % 2, :], silu[:, q % 2, :], wrow[:, (e - 1) % 2, :],
                                       op=ALU.mult).then_inc(sw_ok, 1)

            chunk(0)
            with pool.Fori(1, NCH, 1) as c:
                chunk(c)

        @block.scalar
        def _(act):
            def evac_heads(b, half):
                act.wait_ge(pv_ok, b * G + 2 * half + 2)
                if half == 0 and (not isinstance(b, int) or b >= 1):
                    act.wait_ge(un_ok, b * TT)
                act.activation(UT[:, 2 * half:2 * half + 2, :], ps[:, PU, :].rearrange("p (g t) -> p g t", g=2),
                               ACT.Copy).then_inc(ut_ok, 1)

            def iteration(i, ph, has, _):
                front, _, scores, tail, gates = has
                if front:
                    f = i + 2
                    act.wait_ge(xt_ok, f + 1)
                    if not isinstance(i, int) or f >= 1:
                        act.wait_ge(v_ok, f)
                    act.activation(xnT[:, :], ps[:, PM + 1, 0:S], ACT.Copy).then_inc(xnT_ok, 1)
                if tail:
                    evac_heads(i - 1, 1)

                def hi_part():
                    f = i + 2
                    act.wait_ge(rot_ok, f + 1)
                    if not isinstance(i, int) or f >= 1:
                        for g in range(G):
                            act.wait_ge(qk_ok[g], 16 * STACKS * f)
                    act.activation(HL[:, :, 0, :], rc[:, :, :], ACT.Copy).then_inc(hi_ok, 1)

                def second_norm():
                    t = i - 2
                    act.wait_ge(xt2_ok, t + 1)
                    if not isinstance(i, int) or t >= 1:
                        act.wait_ge(xl_ok, t)
                    act.activation(xf[:, :], ps[:, PM + 1, 0:S], ACT.Copy).then_inc(xf_ok, 1)
                    act.wait_ge(xf_ok, t + 1)
                    act.activation(XH[:, bass.ds(t * S, S)], xf[:, :], ACT.Copy).then_inc(xh_ok, 1)

                def gate_exp():
                    t = i - 2
                    act.wait_ge(g_ok, t + 1)
                    act.activation(GE[:, tiles(t), :], ps[:, PM, 0:TT * NE].rearrange("p (a e) -> p a e", a=TT),
                                   ACT.Exp, scale=-1.0).then_inc(ge_ok, 1)

                def att_evac():
                    t = i - 1
                    act.wait_ge(at_ok, t + 1)
                    act.activation(attT[:, :], ps[:, PM + 1, 0:S], ACT.Copy).then_inc(atT_ok, 1)

                after = {}
                if front:
                    after[4] = hi_part
                if gates:
                    after[14] = second_norm
                    after[15] = gate_exp
                if tail:
                    after[11] = att_evac
                for h in range(H):
                    if scores:
                        n = i * H + h
                        act.wait_ge(sb_ok, n + 1)
                        if h % G == 0 and (not isinstance(i, int) or H * i + h >= 8):
                            act.wait_ge(pv_ok, i * G + h // G - 1)
                        act.activation(PR[:, h % 8, :, :],
                                       ps[:, SB + (ph + h) % 3, :].rearrange("p (a t) -> p a t", a=TT),
                                       ACT.Exp, scale=SCALE).then_inc(ex_ok, 1)
                        if h == 10:
                            evac_heads(i, 0)
                    if h in after:
                        after[h]()

            run(act, iteration)

            act.wait_ge(sb_ok, NB * H)
            act.wait_ge(pv_ok, NB * G)
            act.wait_ge(un_ok, NB * TT)

            def hidden_hi(n, q):
                if not isinstance(n, int) or n >= 3:
                    act.wait_ge(dn_ok, n - 2)
                act.wait_ge(h_ok, n + 1)
                act.activation(hid_part[:, q % 3, 0, :], hid[:, q % 2, :], ACT.Copy).then_inc(hh_ok, 1)

            def sum_out(c):
                if not isinstance(c, int) or c >= 1:
                    act.wait_ge(y_t, c)
                act.wait_ge(dn_ok, c * HV + HV)
                act.activation(yT, ps[:, Y0, :], ACT.Copy).then_inc(yT_ok, 1)

            def chunk(c):
                dyn = not isinstance(c, int)
                for q in range(HV):
                    n = c * HV + q
                    if dyn or n >= 2:
                        act.wait_ge(h_ok, n - 1)
                    act.wait_ge(gu_ok, n + 1)
                    act.activation(silu[:, q % 2, :], ps[:, G0 + q % 2, :], ACT.Silu).then_inc(si_ok, 1)
                    if dyn or n >= 1:
                        hidden_hi(n - 1, (q - 1) % HV)
                    if q % 2 and q // 2 < NE:
                        e = q // 2 + 1
                        m = c * NE + e
                        if dyn or m >= 3:
                            act.wait_ge(sw_ok, (m - 2) * FH)
                        act.wait_ge(wb_t, m)
                        act.activation(wrow[:, (e - 1) % 2, :], ps[:, wrow_bank(e), :], ACT.Copy).then_inc(wb_ok, 1)
                    if q == 1 and (dyn or c >= 1):
                        sum_out(c - 1)

            chunk(0)
            with act.Fori(1, NCH, 1) as c:
                chunk(c)
            hidden_hi(NCH * HV - 1, HV - 1)
            sum_out(NCH - 1)

        @block.vector
        def _(dve):
            dve.memset(halves[:, :], -0.5).then_inc(setup_dve, 1)
            for n in range(NBUF):
                dve.memset(QK[KA:P, n, 1, :, :].bitcast(F32), 1.0).then_inc(setup_dve, 1)

            def norm_stats(src, st, s_st):
                for a in range(TT):
                    last = dve.bn_stats(st[:, a, :], src[:, a, :])
                last.then_inc(s_st, 1)

            def norm_mean(b, st, m, v, s_mv, done):
                for a in range(TT):
                    last = dve.bn_aggr(m[:, a, :], st[:, a, :])
                last.then_inc(s_mv, 1)
                dve.wait_ge(s_mv, b + 1)
                dve.tensor_scalar(v[:, :], m[:, :, 1:2].rearrange("p a o -> p (a o)"), EPS, None,
                                  ALU.add).then_inc(done, 1)

            def norm_apply(src, dst, b, m, r, s_rs, done):
                dve.wait_ge(s_rs, b + 1)
                for a in range(TT):
                    last = dve.tensor_scalar(dst[:, a, :], src[:, a, :], m[:, a, 0:1], r[:, a:a + 1],
                                             ALU.subtract, ALU.mult)
                last.then_inc(done, 1)

            def first_apply(f, static):
                if not static:
                    dve.wait_ge(xt_ok, f)
                norm_apply(X[:, tiles(f), :], xn, f, mv, rstd, rs1, xn_ok)

            dve.wait_ge(xld[0], 16)
            norm_stats(X[:, tiles(0), :], stat, st1)
            dve.wait_ge(st1, 1)
            norm_mean(0, stat, mv, veps, mv1, ve1)
            first_apply(0, True)
            dve.wait_ge(cst_ld, 16)
            dve.wait_ge(bcol_ld, 16)

            steps = [0]

            def step(ins):
                steps[0] += 1
                ins.then_inc(rt, 1)
                dve.wait_ge(rt, steps[0])

            def route(t0, t1):
                n = t1 - t0
                gate, rank, wsel, wpart, beats, beats_flat = routing_tiles(n)
                wsum, wrec = GE[:, t0:t1, 0:1], GE[:, t0:t1, 1:2]
                dve.wait_ge(ge_ok, t1 // TT)
                step(dve.tensor_scalar(gate, GE[:, t0:t1, :], 1.0, None, ALU.add))
                step(dve.reciprocal(gate, gate))
                dve.memset(beats_flat[:, :, 0:NE * NE:NE + 1], 0.0)
                for j in range(NE):
                    for e0, e1, op in ((0, j, ALU.is_gt), (j + 1, NE, ALU.is_ge)):
                        if e0 < e1:
                            last = dve.tensor_tensor(beats[:, :, e0:e1, j], gate[:, :, j:j + 1].broadcast_to([P, n, e1 - e0]),
                                                     gate[:, :, e0:e1], op=op)
                step(last)
                step(dve.tensor_reduce(rank, beats, op=ALU.add, axis=AX.X))
                step(dve.scalar_tensor_tensor(wsel, rank, 2.0, gate, op0=ALU.is_lt, op1=ALU.mult))
                step(dve.tensor_reduce(wsum, wsel, op=ALU.add, axis=AX.X))
                step(dve.reciprocal(wrec, wsum))
                step(dve.scalar_tensor_tensor(wpart, wsel, 1.0 / 3.0, wrec.broadcast_to([P, n, NE]),
                                              op0=ALU.mult, op1=ALU.mult))
                step(dve.tensor_copy(WHL[:, t0:t1, 0, :], wpart))
                step(dve.tensor_tensor(WHL[:, t0:t1, 1, :], wpart, WHL[:, t0:t1, 0, :].bitcast(F32), op=ALU.subtract))

            def iteration(i, ph, has, lowest):
                front, maxima, scores, tail, gates = has
                more = front and (not isinstance(i, int) or i + 3 < NB)

                def reduce(u):
                    if not maxima:
                        return
                    a = i + 1
                    if u == 0 and (not isinstance(i, int) or a >= 1):
                        dve.wait_ge(ml_ok, a)
                    dve.wait_ge(sa_ok, a * H + u + 1)
                    hp, qt = u // 2, u % 2
                    dve.tensor_reduce(MX[:, qt, 2 * hp:2 * hp + 2],
                                      ps[:, SA + u % 2, :].rearrange("p (h k) -> p h k", h=2),
                                      op=ALU.max, axis=AX.X).then_inc(mx_ok, 1)

                def rope_mul(n, wait, bank_, done):
                    f = i + 2
                    dve.wait_ge(wait, f + 1)
                    if n == 0 and (not isinstance(i, int) or f >= 1):
                        dve.wait_ge(lo_ok, f)
                    dve.scalar_tensor_tensor(rc[:, n, :], ps[:, PM + bank_, 0:S], bcol[:, 2 * n:2 * n + 1],
                                             rope[:, 0, :], op0=ALU.add, op1=ALU.mult)
                    dve.scalar_tensor_tensor(rs[:, n, :], ps[:, PM + bank_, S:2 * S], bcol[:, 2 * n + 1:2 * n + 2],
                                             rope[:, 1, :], op0=ALU.add, op1=ALU.mult).then_inc(done, 1)

                def values():
                    f, pf = i + 2, (ph + 2) % NBUF
                    if isinstance(i, int) and f == 0:
                        dve.wait_ge(ld, 16 * NLD)
                        dve.wait_ge(setup_pool, 2)
                    dve.wait_ge(v_ok, f + 1)
                    if not isinstance(i, int) or i >= 1:
                        dve.wait_ge(pv_ok, i * G)
                    dve.tensor_tensor(VX[:, pf, :, :, 0:DH],
                                      ps[:, PM, 0:S].rearrange("p (a h d) -> p a h d", a=TT, h=H),
                                      brow[:, 0:1, :].rearrange("p o (h d) -> p o h d", h=H)
                                      .broadcast_to([P, TT, H, DH]), op=ALU.add).then_inc(vx_ok, 1)

                def statistics():
                    if isinstance(i, int) and i < 0:
                        for n in ((1,) if i == -2 else (2, 3)):
                            dve.wait_ge(xld[n], 16)
                    norm_stats(X[:, tiles(i + 3), :], stat, st1)
                    dve.wait_ge(st1, i + 4)

                def means():
                    norm_mean(i + 3, stat, mv, veps, mv1, ve1)

                def normalise(a):
                    t = i - 1
                    bk_ = PM + 1 - a
                    u = ps[:, bk_, :].rearrange("p (h c) -> p h c", h=H)
                    dve.wait_ge(un_ok, t * TT + a + 1)
                    dve.reciprocal(rden[:, a, :], u[:, :, DH:DH + 1].rearrange("p h o -> p (h o)")).then_inc(rd_ok, 1)
                    dve.wait_ge(rd_ok, t * TT + a + 1)
                    if a == 0 and (not isinstance(i, int) or t >= 1):
                        dve.wait_ge(at_ok, t)
                    dve.tensor_tensor(att[:, a, :].rearrange("p (h d) -> p h d", h=H), u[:, :, 0:DH],
                                      rden[:, a, :].rearrange("p (h o) -> p h o", o=1).broadcast_to([P, H, DH]),
                                      op=ALU.mult).then_inc(att_ok, 1)

                def second_apply():
                    if not gates:
                        return
                    gt = i - 2
                    if not isinstance(i, int) or gt >= 1:
                        dve.wait_ge(xt2_ok, gt)
                    norm_apply(X[:, tiles(gt), :], xn2, gt, mv2, rstd2, rs2, xn2_ok)

                def residual():
                    t = i - 1
                    dve.wait_ge(wo_ok, t + 1)
                    dve.wait_ge(bo_ok, t + 1)
                    dve.tensor_tensor(X[:, tiles(t), :], ps[:, PM, 0:S].rearrange("p (a d) -> p a d", a=TT),
                                      X[:, tiles(t), :], op=ALU.add).then_inc(x2_ok, 1)

                def split_maxima():
                    a = i + 1
                    if tail:
                        dve.wait_ge(x2_ok, i)
                    if maxima:
                        dve.wait_ge(mx_ok, a * H + H)
                        if not isinstance(i, int) or a >= 1:
                            dve.wait_ge(mt_ok, a)
                        m = MX[:, :, :].rearrange("p a (g j) -> p a g j", g=G)
                        dve.tensor_scalar(MHL[:, :, :, 0, :], m, -1.0, None, ALU.mult).then_inc(mh_ok, 1)
                        dve.wait_ge(mh_ok, a + 1)
                        for qt in range(TT):
                            last = dve.scalar_tensor_tensor(
                                MHL[:, qt, :, 1, :], m[:, qt, :, :], -1.0, MHL[:, qt, :, 0, :].bitcast(F32),
                                op0=ALU.mult, op1=ALU.subtract)
                        last.then_inc(ml_ok, 1)

                if scores:
                    reduce(0)
                    dve.wait_ge(mt_ok, i + 1)
                    if not isinstance(i, int) or i >= 1:
                        for g in range(G):
                            dve.wait_ge(sh_ok[g], 16 * i)
                    dve.tensor_copy(MT[:, :], ps[0:32, PM, 0:S]).then_inc(mts_ok, 1)
                if isinstance(i, int) and i == NB - 1:
                    dve.wait_ge(pv_ok, (NB - 1) * G)
                    route(0, NT // 2)
                if isinstance(i, int) and i == NB:
                    route(NT // 2, NT - 2 * TT)
                if isinstance(i, int) and i == NB + 1:
                    dve.wait_ge(sb_ok, NB * H)
                    dve.tensor_tensor(SEL, ident[0:2 * NE, 0:NE].rearrange("p (e o) -> p e o", o=1)
                                      .broadcast_to([2 * NE, NE, P]),
                                      ident[0:2 * NE, NE:2 * NE].rearrange("p (e o) -> p e o", o=1)
                                      .broadcast_to([2 * NE, NE, P]), op=ALU.add).then_inc(sel_ok, 1)
                front_first = front and not scores
                if front_first:
                    rope_mul(0, q_ok, 0, rq_ok)
                    rope_mul(1, k_ok, 1, rk_ok)
                    values()
                    statistics()
                    means()
                    reduce(0)
                reduce(1); reduce(2); reduce(3)
                if front and not front_first:
                    rope_mul(0, q_ok, 0, rq_ok)
                reduce(4)
                if front and not front_first:
                    rope_mul(1, k_ok, 1, rk_ok)
                reduce(5)
                if front and not front_first:
                    values()
                    if more:
                        statistics()
                if gates:
                    dve.wait_ge(st2, i - 1)
                reduce(6)
                if more and not front_first:
                    means()
                if gates:
                    norm_mean(i - 2, stat2, mv2, veps2, mvs2, ve2)
                reduce(7); reduce(8)
                if tail:
                    normalise(0)
                reduce(9)
                if tail:
                    normalise(1)
                reduce(10)
                if more:
                    first_apply(i + 3, False)
                reduce(11)
                second_apply()
                reduce(12); reduce(13); reduce(14)
                if tail:
                    residual()
                reduce(15)
                split_maxima()
                if tail:
                    norm_stats(X[:, tiles(i - 1), :], stat2, st2)

            run(dve, iteration)

            def hidden_lo(n, q):
                dve.wait_ge(hh_ok, n + 1)
                dve.tensor_tensor(hid_part[:, q % 3, 1, :], hid[:, q % 2, :], hid_part[:, q % 3, 0, :].bitcast(F32),
                                  op=ALU.subtract).then_inc(hl_ok, 1)

            def residual(c):
                dve.wait_ge(y_t, c + 1)
                rows = X[:, bass.ds(c * CT, CT), :]
                dve.tensor_tensor(rows, ps[:, M0 + 1, :].rearrange("p (a d) -> p a d", a=CT), rows,
                                  op=ALU.add).then_inc(y_ok, 1)

            def chunk(c):
                dyn = not isinstance(c, int)
                if dyn or c >= 1:
                    dve.wait_ge(wt_t, c)
                dve.tensor_copy(WC[:, :, :], WHL[:, bass.ds(c * CT, CT), :, :].rearrange("p t l e -> p t (l e)")
                                .bitcast(F32)).then_inc(wc_ok, 1)
                for q in range(HV):
                    n = c * HV + q
                    if dyn or n >= 1:
                        hidden_lo(n - 1, (q - 1) % HV)
                    if q < FH:
                        dve.wait_ge(si_ok, n + 1)
                        dve.scalar_tensor_tensor(hid[:, q % 2, :], silu[:, q % 2, :], 1.0 / 3.0, ps[:, U0 + q % 2, :],
                                                 op0=ALU.mult, op1=ALU.mult).then_inc(h_ok, 1)
                    else:
                        dve.wait_ge(sw_ok, c * NE * FH + q - FH + 1)
                        dve.tensor_tensor(hid[:, q % 2, :], silw[:, q % 2, :], ps[:, U0 + q % 2, :],
                                          op=ALU.mult).then_inc(h_ok, 1)
                    if q == 0:
                        if dyn or c >= 1:
                            dve.wait_ge(wb_t, c * NE)
                        dve.wait_ge(wt_t, c + 1)
                        dve.tensor_copy(WT, ps[0:2 * NE, M0, :]).then_inc(wt_ok, 1)
                    if q == 5 and (dyn or c >= 1):
                        residual(c - 1)

            route(NT - 2 * TT, NT)
            chunk(0)
            with dve.Fori(1, NCH, 1) as c:
                chunk(c)
            hidden_lo(NCH * HV - 1, HV - 1)
            residual(NCH - 1)

        @block.tensor
        def _(pe):
            mm = pe.matmul
            pe.wait_ge(cst_ld, 16)

            def heads_out(b, pb, g):
                dyn = not isinstance(b, int)
                pe.wait_ge(ex_ok, b * H + 4 * g + 4)
                if g == 0:
                    pe.wait_ge(vx_ok, b + 1)
                    if dyn or b >= 1:
                        pe.wait_ge(ut_ok, b * 2)
                if g == 2:
                    pe.wait_ge(ut_ok, b * 2 + 1)
                for kt in range(TT):
                    for j in range(J):
                        last = mm(ps[32 * j:32 * j + 32, PU, (g % 2) * S:(g % 2 + 1) * S],
                                  VX[:, pb, kt, G * g + j, :], PR[:, (G * g + j) % 8, kt, :],
                                  start=kt == 0, stop=kt == TT - 1)
                last.then_inc(pv_ok, 1)

            def iteration(i, ph, has, _):
                front, maxima, scores, tail, gates = has
                dyn = not isinstance(i, int)
                f, t, gt = i + 2, i - 1, i - 2
                pa = (ph + 1) % NBUF

                def unit(u):
                    if not maxima:
                        return
                    a = i + 1
                    if u % G == 0:
                        pe.wait_ge(kz_ok, a * G + u // G + 1)
                    n = a * H + u
                    if dyn or n >= 2:
                        pe.wait_ge(mx_ok, n - 1)
                    hp, qt = u // 2, u % 2
                    g, j = hp // 2, 2 * (hp % 2)
                    mm(ps[:, SA + u % 2, :], QK[0:KA, pa, 0, g, qt * P:(qt + 1) * P],
                       KZ[0:KA, pa, g, j:j + 2, :], start=True, stop=True).then_inc(sa_ok, 1)

                def head(h):
                    if not scores:
                        return
                    n = i * H + h
                    if h % J == 0:
                        pe.wait_ge(sh_ok[h // J], (i + 1) * 16)
                    if dyn or n >= 3:
                        pe.wait_ge(ex_ok, n - 2)
                    g, j = h // J, h % J
                    for kt in range(TT):
                        last = mm(ps[:, SB + (ph + h) % 3, kt * S:(kt + 1) * S],
                                  KZ[0:KB, ph, g, j, kt * P:(kt + 1) * P], QK[0:KB, ph, 0, g, :],
                                  start=True, stop=True)
                    last.then_inc(sb_ok, 1)

                def project(n, bank_, done):
                    for s, w in enumerate((wraw[:, 2 * n, :], wraw[:, 2 * n + 1, :])):
                        last = mm(ps[:, PM + bank_, s * S:(s + 1) * S], w, xnT[:, :], start=True, stop=True)
                    last.then_inc(done, 1)

                def back_to_rows(a, bank_):
                    for g in range(G):
                        last = pe.transpose(ps[:, PM + bank_, g * P:(g + 1) * P], UT[:, g, a * P:(a + 1) * P], ident)
                    last.then_inc(un_ok, 1)

                def maxima_rows():
                    if not scores:
                        return
                    pe.wait_ge(ml_ok, i + 1)
                    if dyn or i >= 3:
                        pe.wait_ge(ge_ok, i - 2)
                    elif i == 2:
                        pe.wait_ge(x2_ok, i - 1)
                    else:
                        pe.wait_ge(vx_ok, i + 2)
                    for a in range(TT):
                        last = pe.transpose(ps[0:32, PM, a * P:(a + 1) * P],
                                            MHL[:, a, :, :, :].rearrange("p g l j -> p (g l j)").bitcast(F32), ident)
                    last.then_inc(mt_ok, 1)

                def front_tokens():
                    if not front:
                        return
                    pe.wait_ge(xn_ok, f + 1)
                    if dyn or i >= 3:
                        pe.wait_ge(xf_ok, i - 2)
                    elif i == 2:
                        pe.wait_ge(atT_ok, i - 1)
                    elif i >= -1:
                        pe.wait_ge(rk_ok, f)
                    for a in range(TT):
                        last = pe.transpose(ps[:, PM + 1, a * P:(a + 1) * P], xn[:, a, :], ident)
                    last.then_inc(xt_ok, 1)

                def queries():
                    if not front:
                        return
                    pe.wait_ge(xnT_ok, f + 1)
                    if isinstance(i, int) and i == -2:
                        pe.wait_ge(wqk_ld, 16)
                    if scores:
                        pe.wait_ge(mts_ok, i + 1)
                    elif i == -1:
                        pe.wait_ge(vx_ok, f)
                    project(0, 0, q_ok)

                def keys():
                    if front:
                        project(1, 1, k_ok)

                def values():
                    if not front:
                        return
                    if isinstance(i, int) and i == -2:
                        pe.wait_ge(ld, 16 * NLD)
                    pe.wait_ge(rq_ok, f + 1)
                    for a in range(TT):
                        last = mm(ps[:, PM, a * P:(a + 1) * P], xnT[:, a * P:(a + 1) * P], wraw[:, 4, :],
                                  start=True, stop=True)
                    last.then_inc(v_ok, 1)

                def rows_0():
                    if not tail:
                        return
                    pe.wait_ge(ut_ok, t * 2 + 2)
                    if front:
                        pe.wait_ge(rk_ok, f + 1)
                    else:
                        pe.wait_ge(xf_ok, gt)
                    back_to_rows(0, 1)

                def rows_1():
                    if not tail:
                        return
                    if front:
                        pe.wait_ge(vx_ok, f + 1)
                    elif scores:
                        pe.wait_ge(mts_ok, i + 1)
                    else:
                        pe.wait_ge(ge_ok, gt)
                    back_to_rows(1, 0)

                def attention_T():
                    if not tail:
                        return
                    pe.wait_ge(att_ok, t * TT + TT)
                    for a in range(TT):
                        last = pe.transpose(ps[:, PM + 1, a * P:(a + 1) * P], att[:, a, :], ident)
                    last.then_inc(at_ok, 1)

                def output():
                    if not tail:
                        return
                    pe.wait_ge(atT_ok, t + 1)
                    for a in range(TT):
                        last = mm(ps[:, PM, a * P:(a + 1) * P], attT[:, a * P:(a + 1) * P], wraw[:, 5, :],
                                  start=True, stop=True)
                    last.then_inc(wo_ok, 1)

                def second_tokens():
                    if not gates:
                        return
                    pe.wait_ge(xn2_ok, gt + 1)
                    if tail:
                        pe.wait_ge(atT_ok, t + 1)
                    else:
                        pe.wait_ge(xf_ok, gt)
                    for a in range(TT):
                        last = pe.transpose(ps[:, PM + 1, a * P:(a + 1) * P], xn2[:, a, :], ident)
                    last.then_inc(xt2_ok, 1)

                def gate_logits():
                    if not gates:
                        return
                    pe.wait_ge(xf_ok, gt + 1)
                    if tail:
                        pe.wait_ge(x2_ok, t + 1)
                    else:
                        pe.wait_ge(ge_ok, gt)
                    for a in range(TT):
                        last = mm(ps[:, PM, a * NE:(a + 1) * NE], xf[:, a * P:(a + 1) * P], wg[:, :],
                                  start=True, stop=True)
                    last.then_inc(g_ok, 1)

                def heads(g):
                    if scores:
                        heads_out(i, ph, g)

                if not scores:
                    front_tokens(); queries(); keys(); values()
                unit(0)
                if scores:
                    front_tokens()
                unit(1)
                maxima_rows()
                if tail:
                    heads_out(t, (ph - 1) % NBUF, 3)
                unit(2)
                if scores:
                    queries()
                unit(3)
                if scores:
                    keys()
                unit(4); head(0); head(1)
                if scores:
                    values()
                unit(5); head(2); head(3)
                unit(6); head(4)
                unit(7); head(5); head(6)
                unit(8); heads(0); head(7); rows_0()
                unit(9); head(8); head(9); rows_1()
                unit(10); head(10); heads(1)
                unit(11); head(11); attention_T()
                unit(12); head(12); head(13)
                unit(13); output(); heads(2)
                unit(14); head(14); second_tokens()
                unit(15); head(15); gate_logits()

            run(pe, iteration)

            pe.wait_ge(sel_ok, 1)
            pe.wait_ge(xl_ok, NB)
            pe.wait_ge(ge_ok, NB)
            pe.wait_ge(ut_ok, NB * 2)

            def up(c, q):
                dyn = not isinstance(c, int)
                n = c * HV + q
                e, v = q // FH, q % FH
                if not dyn and c == 0:
                    pe.wait_ge(wl_ok, e + 1)
                if dyn or n >= 2:
                    pe.wait_ge(h_ok, n - 1)
                tok = bass.ds(c * CH, CH)
                for b, w in ((G0, v * P), (U0, F + v * P)):
                    for k, (l, part) in enumerate(((0, XH), (0, XL), (1, XH))):
                        last = mm(ps[:, b + q % 2, :], up_part(e, l)[:, w:w + P], part[:, tok],
                                  start=k == 0, stop=k == 2)
                last.then_inc(gu_ok, 1)

            def down(c, q):
                e, v = q // FH, q % FH
                if q == 0 and (not isinstance(c, int) or c >= 1):
                    pe.wait_ge(yT_ok, c)
                pe.wait_ge(hl_ok, c * HV + q + 1)
                for k, (l, m) in enumerate(((0, 0), (0, 1), (1, 0))):
                    last = mm(ps[:, Y0, :], dn_part(e, l)[:, v, :], hid_part[:, q % 3, m, :],
                              start=q == 0 and k == 0, stop=q == HV - 1 and k == 2)
                last.then_inc(dn_ok, 1)

            def sum_rows(c):
                pe.wait_ge(yT_ok, c + 1)
                for a in range(CT):
                    last = pe.transpose(ps[:, M0 + 1, a * P:(a + 1) * P], yT[:, a * P:(a + 1) * P], ident)
                last.then_inc(y_t, 1)

            def chunk(c):
                dyn = not isinstance(c, int)
                for k in range(NEX):
                    for q in (2 * k, 2 * k + 1):
                        up(c, q)
                        if q >= 2:
                            down(c, q - 2)
                        elif dyn or c >= 1:
                            down(c - 1, HV - 2 + q)
                        if q == 0:
                            if dyn or c >= 1:
                                pe.wait_ge(wb_ok, c * NE - 1)
                            pe.wait_ge(wc_ok, c + 1)
                            for a in range(CT):
                                last = pe.transpose(ps[0:2 * NE, M0, a * P:(a + 1) * P], WC[:, a, :], ident)
                            last.then_inc(wt_t, 1)
                    e = k + 1
                    if e <= NE:
                        if e == 1:
                            pe.wait_ge(wt_ok, c + 1)
                            if dyn or c >= 1:
                                pe.wait_ge(wb_ok, c * NE)
                        elif e == 3:
                            pe.wait_ge(wb_ok, c * NE + 2)
                        elif e == 4 and (dyn or c >= 1):
                            pe.wait_ge(y_ok, c)
                        elif e >= 4:
                            pe.wait_ge(wb_ok, c * NE + e - 2)
                        mm(ps[:, wrow_bank(e), :], SEL[:, e - 1, :], WT, start=True, stop=True).then_inc(wb_t, 1)
                    if k == 1 and (dyn or c >= 1):
                        pe.wait_ge(wb_ok, c * NE + 1)
                        sum_rows(c - 1)

            chunk(0)
            with pe.Fori(1, NCH, 1) as c:
                chunk(c)
            for q in (HV - 2, HV - 1):
                down(NCH - 1, q)
            sum_rows(NCH - 1)


def constants():
    import numpy as np
    c = np.zeros((P, C_ALL), np.float32)
    inv_freq = (1.0 / 10000.0 ** (np.arange(0, DH, 2, dtype=np.float32) / np.float32(DH))).astype(np.float32)
    freqs = np.arange(S, dtype=np.float32)[:, None] * inv_freq[None, :]
    ang = np.concatenate((freqs, freqs), axis=-1)[:, ::2].astype(np.float32)
    for p in range(P):
        a = ang[:, (p % DH) // 2]
        c[p, C_ROPE:C_ROPE + S] = np.cos(a)
        c[p, C_ROPE + S:C_ROPE + 2 * S] = np.sin(a) if p % 2 else -np.sin(a)
        c[p, C_IDENT + p] = 1.0
        if p < KA:
            c[p, C_MASK + p % 32 // DH] = 1.0
        elif p < KB:
            c[p, C_MASK + p % J] = 1.0
    return c


def kernel(L0_attn_x, L0_attn_Wq, L0_attn_bq, L0_attn_Wk, L0_attn_bk, L0_attn_Wv, L0_attn_bv, L0_attn_Wo, L0_attn_bo,
           L0_ffn_Wg, L0_ffn_Ws1, L0_ffn_Ws3, L0_ffn_Ws2, L0_ffn_We1, L0_ffn_We3, L0_ffn_We2):
    import numpy as np
    import concourse.bacc as bacc
    from concourse.bass_utils import run_bass_kernel_spmd

    def swapped(a):
        a = np.asarray(a)
        return a.reshape(a.shape[:-1] + (a.shape[-1] // 2, 2))[..., ::-1].reshape(a.shape)

    w_att = np.concatenate([np.asarray(L0_attn_Wq), swapped(L0_attn_Wq), np.asarray(L0_attn_Wk),
                            swapped(L0_attn_Wk), np.asarray(L0_attn_Wv), np.asarray(L0_attn_Wo)], axis=1)
    b_cols = np.stack([np.asarray(L0_attn_bq), swapped(L0_attn_bq), np.asarray(L0_attn_bk), swapped(L0_attn_bk)], axis=1)
    w1 = np.concatenate([np.asarray(L0_ffn_Ws1)[None], np.asarray(L0_ffn_We1)])
    w3 = np.concatenate([np.asarray(L0_ffn_Ws3)[None], np.asarray(L0_ffn_We3)])
    w2 = np.concatenate([np.asarray(L0_ffn_Ws2)[None], np.asarray(L0_ffn_We2)])
    w_up = np.concatenate([w1, w3], axis=2).transpose(1, 0, 2)
    w_down = w2.reshape(NEX, FH, P, D).transpose(2, 0, 1, 3)

    nc = bacc.Bacc("TRN2", target_bir_lowering=False, num_devices=1)
    arrays, args = {}, []
    for name, a in (("x", L0_attn_x), ("w_att", w_att), ("b_cols", b_cols), ("bv", L0_attn_bv), ("bo", L0_attn_bo),
                    ("Wg", L0_ffn_Wg), ("w_up", w_up), ("w_down", w_down), ("const", constants())):
        a = np.ascontiguousarray(a)
        arrays[f"in_{name}"] = a
        args.append(nc.dram_tensor(f"in_{name}", a.shape, mybir.dt.from_np(a.dtype), kind="ExternalInput").ap())
    args.append(nc.dram_tensor("out_0", (NB, S, D), F32, kind="ExternalOutput").ap())
    layer_kernel(nc, *args)
    r = run_bass_kernel_spmd(nc, [arrays], core_ids=[0])
    return r.results[0]["out_0"]
```

```python
from contextlib import ExitStack

import concourse.bass as bass
from concourse import mybir

ALU = mybir.AluOpType
ACT = mybir.ActivationFunctionType
AX = mybir.AxisListType
F32 = mybir.dt.float32
F32R = mybir.dt.float32r

P = 128
NB = 16
S = 256
D = 128
H = 16
DH = 8
G = 4
J = 4
TT = S // P
NT = NB * TT
F = 256
FH = F // P
NE = 8
NEX = NE + 1
CH = 512
NCH = NB * S // CH
CT = CH // P
KA = 96
KB = 104
NBUF = 3
SCALE = float(DH) ** -0.5
EPS = 1e-5

C_ROPE = 0
C_IDENT = C_ROPE + 2 * S
C_MASK = C_IDENT + P
C_ALL = C_MASK + J


def layer_kernel(nc, x, w_att, b_cols, bv, bo, Wg, w_up, w_down, const, out):
    with ExitStack() as ctx:
        def sb(name, shape, dt=F32):
            return ctx.enter_context(nc.sbuf_tensor(name, shape, dt))

        def sem(name):
            return ctx.enter_context(nc.semaphore(name))

        X = sb("X", [P, NT, D])
        cst = sb("cst", [P, C_ALL])
        wraw = sb("wraw", [P, 6, D])
        wg = sb("wg", [P, NE])
        bcol = sb("bcol", [P, 4])
        brow = sb("brow", [P, 2, D])
        stat = sb("stat", [P, TT, 6])
        mv = sb("mv", [P, TT, 2])
        veps = sb("veps", [P, TT])
        rstd = sb("rstd", [P, TT])
        nmean = sb("nmean", [P, TT])
        nbias = sb("nbias", [P, TT])
        nmean2 = sb("nmean2", [P, TT])
        nbias2 = sb("nbias2", [P, TT])
        halves = sb("halves", [P, TT])
        silu_table = sb("silu_table", [P, 1])
        stat2 = sb("stat2", [P, TT, 6])
        mv2 = sb("mv2", [P, TT, 2])
        veps2 = sb("veps2", [P, TT])
        rstd2 = sb("rstd2", [P, TT])
        xn = sb("xn", [P, TT, D])
        xn2 = sb("xn2", [P, TT, D])
        xnT = sb("xnT", [P, S])
        rc = sb("rc", [P, 2, S])
        rs = sb("rs", [P, 2, S])
        HL = sb("HL", [P, 2, 2, S], F32R)
        QK = sb("QK", [P, NBUF, 2, G, S], F32R)
        KZ = sb("KZ", [P, NBUF, G, J, S], F32R)
        VX = sb("VX", [P, NBUF, TT, H, 32])
        MX = sb("MX", [P, TT, H])
        MHL = sb("MHL", [P, TT, G, 2, J], F32R)
        MT = sb("MT", [32, S], F32R)
        PR = sb("PR", [P, 8, TT, S])
        UT = sb("UT", [P, G, S])
        rden = sb("rden", [P, TT, H])
        att = sb("att", [P, TT, D])
        attT = sb("attT", [P, S])
        xf = sb("xf", [P, S])
        XH = sb("XH", [P, NB * S], F32R)
        XL = sb("XL", [P, NB * S], F32R)
        GE = sb("GE", [P, NT, NE])
        WHL = sb("WHL", [P, NT, 2, NE], F32R)
        WC = sb("WC", [P, CT, 2 * NE])
        up_raw = sb("up_raw", [P, NEX, 2 * F])
        dn_raw = sb("dn_raw", [P, NEX, FH, D])
        kz_flat = KZ[:, :, :, :, :].rearrange("p n g j t -> p (n g j t)")
        qk_flat = QK[:, :, :, :, :].rearrange("p n a g t -> p (n a g t)")
        UPW, DNW = 2 * 2 * F, 2 * FH * D
        HIDW = 3 * 2 * CH
        KZ1, QK1 = G * J * S, 2 * G * S

        def up_part(e, l):
            at = KZ1 + e * UPW if e < NE else HIDW
            return kz_flat[:, at + l * 2 * F:at + (l + 1) * 2 * F]

        def dn_part(e, l):
            at = QK1 + e * DNW if e < NE else NE * P + CH
            return qk_flat[:, at + l * FH * D:at + (l + 1) * FH * D].rearrange("p (v d) -> p v d", v=FH)

        hid_part = kz_flat[:, 0:HIDW].rearrange("p (n l t) -> p n l t", n=3, l=2)
        SEL = qk_flat[0:2 * NE, 0:NE * P].rearrange("p (e m) -> p e m", e=NE)
        WT = qk_flat[0:2 * NE, NE * P:NE * P + CH]
        work = PR[:, :, :, :].rearrange("p n a t -> p n (a t)")
        silu, act_up, hid, wrow = work[:, 0:2, :], work[:, 2:4, :], work[:, 4:6, :], work[:, 6:8, :]
        yT = UT[:, :, :].rearrange("p g t -> p (g t)")[:, 0:CH]
        vx_flat = VX[:, :, :, :, :].rearrange("p n a h c -> p (n a h c)")

        def routing_tiles(n):
            at = TT * H * 32
            four = [vx_flat[:, at + k * n * NE:at + (k + 1) * n * NE].rearrange("p (t e) -> p t e", t=n)
                    for k in range(4)]
            flat = vx_flat[:, at + 4 * n * NE:at + (4 + NE) * n * NE]
            return four + [flat.rearrange("p (t e j) -> p t e j", t=n, e=NE),
                           flat.rearrange("p (t k) -> p t k", t=n)]

        ps = ctx.enter_context(nc.psum_tensor("ps", [P, 8, 512], F32))
        SA, SB, PU, PM = 0, 2, 5, 6

        cst_ld = sem("cst_ld")
        wqk_ld = sem("wqk_ld")
        bcol_ld = sem("bcol_ld")
        ld = sem("ld")
        wld = sem("wld")
        xld = [sem(f"xld{n}") for n in range(4)]
        setup_dve = sem("setup_dve")
        setup_pool = sem("setup_pool")
        ve1 = sem("ve1"); ve2 = sem("ve2"); st1 = sem("st1"); mv1 = sem("mv1"); rs1 = sem("rs1")
        rr1 = sem("rr1"); rr2 = sem("rr2")
        st2 = sem("st2"); mvs2 = sem("mvs2"); rs2 = sem("rs2")
        xn_ok = sem("xn_ok")
        xn2_ok = sem("xn2_ok")
        xt_ok = sem("xt_ok")
        xnT_ok = sem("xnT_ok")
        q_ok = sem("q_ok"); k_ok = sem("k_ok"); v_ok = sem("v_ok")
        rq_ok = sem("rq_ok"); rk_ok = sem("rk_ok")
        vx_ok = sem("vx_ok")
        bo_ok = sem("bo_ok")
        rot_ok = sem("rot_ok"); hi_ok = sem("hi_ok"); lo_ok = sem("lo_ok")
        qk_ok = [sem(f"qk_ok{g}") for g in range(G)]
        kz_ok = sem("kz_ok")
        sa_ok = sem("sa_ok")
        mx_ok = sem("mx_ok")
        mh_ok = sem("mh_ok"); ml_ok = sem("ml_ok")
        mt_ok = sem("mt_ok")
        mts_ok = sem("mts_ok")
        sh_ok = [sem(f"sh_ok{g}") for g in range(G)]
        sb_ok = sem("sb_ok")
        ex_ok = sem("ex_ok")
        pv_ok = sem("pv_ok")
        ut_ok = sem("ut_ok")
        un_ok = sem("un_ok")
        rd_ok = sem("rd_ok")
        att_ok = sem("att_ok")
        at_ok = sem("at_ok")
        atT_ok = sem("atT_ok")
        wo_ok = sem("wo_ok")
        x2_ok = sem("x2_ok")
        xt2_ok = sem("xt2_ok"); xf_ok = sem("xf_ok"); xh_ok = sem("xh_ok"); xl_ok = sem("xl_ok")
        g_ok = sem("g_ok")
        ge_ok = sem("ge_ok")

        wh_ok = sem("wh_ok"); wl_ok = sem("wl_ok")
        sel_ok = sem("sel_ok")
        rt = sem("rt")
        wc_ok = sem("wc_ok"); wt_t = sem("wt_t"); wt_ok = sem("wt_ok")
        wb_t = sem("wb_t"); wb_ok = sem("wb_ok")
        gu_ok = sem("gu_ok")
        si_ok = sem("si_ok")
        su_ok = sem("su_ok")
        h_ok = sem("h_ok")
        hh_ok = sem("hh_ok"); hl_ok = sem("hl_ok")
        dn_ok = sem("dn_ok")
        yT_ok = sem("yT_ok"); y_t = sem("y_t"); y_ok = sem("y_ok")
        out_ok = sem("out_ok")

        HV = NEX * FH
        LAG = 3
        G0, U0, Y0, M0 = 0, 2, 4, 5

        rope = cst[:, C_ROPE:C_ROPE + 2 * S].rearrange("p (a t) -> p a t", a=2)
        ident = cst[:, C_IDENT:C_IDENT + P]

        def mask(j):
            return cst[:, C_MASK + j:C_MASK + j + 1]

        x_v = x.rearrange("b (a p) d -> p (b a) d", p=P)
        out_v = out.rearrange("b (a p) d -> p (b a) d", p=P)
        XLOADS = (0, 2, 4, 16, NT)
        NLD = 4
        STACKS = 3

        def wrow_bank(e):
            return M0 + (e % 2 if e < 3 else (e + 1) % 2)

        def tiles(b):
            return bass.ds(b * TT, TT)

        def stages(i):
            return (0 <= i + 2 < NB, 0 <= i + 1 < NB, 0 <= i < NB, 0 <= i - 1 < NB, 0 <= i - 2 < NB)

        def run(eng, iteration):
            first = NBUF
            turns = (NB - 3 - first) // NBUF
            for i in range(-2, first):
                iteration(i, i % NBUF, stages(i))
            with eng.Fori(first, first + (turns - 1) * NBUF + 1, NBUF) as base:
                for r in range(NBUF):
                    iteration(base + r, (first + r) % NBUF, (True,) * 5)
            for i in range(first + turns * NBUF, NB + 2):
                iteration(i, i % NBUF, stages(i))

        block = ctx.enter_context(nc.Block())

        @block.sync
        def _(sp):
            def load_tokens(n):
                lo, hi = XLOADS[n:n + 2]
                sp.dma_start(X[:, lo:hi, :], x_v[:, lo:hi, :]).then_inc(xld[n], 16)

            load_tokens(0)
            sp.dma_start(cst[:, :], const).then_inc(cst_ld, 16)
            sp.dma_start(wraw[:, 0:4, :], w_att[:, 0:4 * D].rearrange("p (n d) -> p n d", n=4)).then_inc(wqk_ld, 16)
            sp.dma_start(bcol[:, :], b_cols).then_inc(bcol_ld, 16)
            load_tokens(1)
            sp.dma_start(wraw[:, 4:6, :], w_att[:, 4 * D:6 * D].rearrange("p (n d) -> p n d", n=2)).then_inc(ld, 16)
            for n, b in enumerate((bv, bo)):
                sp.dma_start(brow[:, n, :], b.rearrange("(o d) -> o d", o=1).broadcast_to([P, D])).then_inc(ld, 16)
            sp.dma_start(wg[:, :], Wg).then_inc(ld, 16)
            load_tokens(2)

            def iteration(i, ph, has):
                front, _, scores, _, _ = has
                if scores:
                    sp.wait_ge(mts_ok, i + 1)
                    for g in range(G):
                        sp.dma_start(QK[KA:KB, ph, 0, g, :].bitcast(F32), MT[8 * g:8 * g + 8, :].bitcast(F32)).then_inc(sh_ok[g], 16)
                if front:
                    f, pf = i + 2, (ph + 2) % NBUF
                    flat = HL[:, :, :, :].rearrange("p a b t -> p (a b) t")

                    def stack(g, r):
                        q, k = ((0, 2), (1, 2), (0, 3))[r]
                        sp.dma_start(QK[32 * r:32 * r + 32, pf, :, g, :].bitcast(F32),
                                     flat[32 * g:32 * g + 32, q:k + 1:k - q, :].bitcast(F32)).then_inc(qk_ok[g], 16)

                    sp.wait_ge(hi_ok, f + 1)
                    for g in range(2):
                        stack(g, 0)
                    sp.wait_ge(lo_ok, f + 1)
                    for g in range(G):
                        for r in range(1 if g < 2 else 0, 3):
                            stack(g, r)
                if isinstance(i, int) and i == -2:
                    load_tokens(3)
                if not isinstance(i, int):
                    e = bass.ds(i - NBUF, 1)
                    sp.dma_start(up_raw[:, e, :], w_up[:, e, :]).then_inc(wld, 16)
                    sp.dma_start(dn_raw[:, e, :, :], w_down[:, e, :, :]).then_inc(wld, 16)

            run(sp, iteration)

            def store(c):
                sp.wait_ge(y_ok, c + 1)
                sp.dma_start(out_v[:, bass.ds(c * CT, CT), :], X[:, bass.ds(c * CT, CT), :]).then_inc(out_ok, 16)

            with sp.Fori(0, NCH, 1) as c:
                store(c)
            sp.wait_ge(out_ok, 16 * NCH)

        @block.gpsimd
        def _(pool):
            pool.memset(VX[:, :, :, :, :], 0.0).then_inc(setup_pool, 1)
            pool.wait_ge(setup_pool, 1)
            pool.memset(VX[:, :, :, :, DH:DH + 1], 1.0).then_inc(setup_pool, 1)
            pool.wait_ge(setup_dve, 1)

            def root(b, v, m, r, n, ready, half, done):
                pool.wait_ge(ready, b + 1)
                pool.tensor_tensor(r[:, :], v[:, :], halves[:, :], op=ALU.pow).then_inc(half, 1)
                pool.wait_ge(half, b + 1)
                pool.tensor_tensor(n[:, :], m[:, :], r[:, :], op=ALU.mult).then_inc(done, 1)

            def first_root(b):
                root(b, veps, nmean, rstd, nbias, ve1, rr1, rs1)

            first_root(0)
            pool.wait_ge(setup_dve, NBUF + 1)
            pool.wait_ge(cst_ld, 16)

            def split_weights(e):
                pool.tensor_scalar(up_part(e, 0), up_raw[:, e, :], 1.0, 1.0, ALU.mult, ALU.mult)
                pool.tensor_scalar(dn_part(e, 0), dn_raw[:, e, :, :], 1.0, 1.0, ALU.mult, ALU.mult).then_inc(wh_ok, 1)
                pool.wait_ge(wh_ok, e + 1)
                pool.tensor_tensor(up_part(e, 1), up_raw[:, e, :], up_part(e, 0).bitcast(F32), op=ALU.subtract)
                pool.tensor_tensor(dn_part(e, 1), dn_raw[:, e, :, :], dn_part(e, 0).bitcast(F32),
                                   op=ALU.subtract).then_inc(wl_ok, 1)

            def add_bias(f):
                if isinstance(f, int) and f == 0:
                    pool.wait_ge(ld, 16 * NLD)
                pool.wait_ge(xn_ok, f + 1)
                pool.tensor_tensor(X[:, tiles(f), :], X[:, tiles(f), :],
                                   brow[:, 1:2, :].broadcast_to([P, TT, D]), op=ALU.add).then_inc(bo_ok, 1)

            def rotate(f):
                pool.wait_ge(rk_ok, f + 1)
                pool.wait_ge(rq_ok, f + 1)
                pool.tensor_tensor(rc[:, :, :], rc[:, :, :], rs[:, :, :], op=ALU.add).then_inc(rot_ok, 1)

            def low_part(f):
                pool.wait_ge(hi_ok, f + 1)
                pool.tensor_tensor(HL[:, :, 1, :], rc[:, :, :], HL[:, :, 0, :].bitcast(F32),
                                   op=ALU.subtract).then_inc(lo_ok, 1)

            def pad_keys(f, pf, g):
                pool.wait_ge(qk_ok[g], 16 * STACKS * (f + 1))
                pool.tensor_tensor(KZ[:, pf, g, 0, :], QK[:, pf, 1, g, :].bitcast(F32),
                                   mask(0).broadcast_to([P, S]), op=ALU.mult)
                for j in range(1, J):
                    last = pool.tensor_scalar(KZ[:, pf, g, j, :], QK[:, pf, 1, g, :].bitcast(F32),
                                              mask(j), 1.0, ALU.mult, ALU.mult)
                last.then_inc(kz_ok, 1)

            def low_tokens(t):
                pool.wait_ge(xh_ok, t + 1)
                tok = bass.ds(t * S, S)
                pool.tensor_tensor(XL[:, tok], xf[:, :], XH[:, tok].bitcast(F32),
                                   op=ALU.subtract).then_inc(xl_ok, 1)

            def iteration(i, ph, has):
                front, _, _, _, gates = has
                dyn = not isinstance(i, int)
                if gates:
                    if dyn or i >= 3:
                        pool.wait_ge(xn2_ok, i - 2)
                    root(i - 2, veps2, nmean2, rstd2, nbias2, ve2, rr2, rs2)
                if dyn or -1 <= i < NB - 3:
                    pool.wait_ge(xn_ok, i + 3)
                    first_root(i + 3)
                if not dyn and i == -2:
                    pool.wait_ge(xn_ok, 1)
                    first_root(1)
                f, pf = i + 2, (ph + 2) % NBUF
                if front and (dyn or i != -1):
                    rotate(f)
                    low_part(f)
                if front:
                    add_bias(f)
                if not dyn and i == -2:
                    rotate(1)
                if dyn or i >= 3:
                    low_tokens(i - 3)
                if not dyn and NB - 2 <= i <= NB:
                    pool.wait_ge(sb_ok, i * H)
                    if i == NB - 2:
                        pool.wait_ge(wld, 16 * 2 * NEX)
                    per = NE // 2
                    for e in range((i - NB + 2) * per, min((i - NB + 3) * per, NEX)):
                        split_weights(e)
                if front:
                    for g in range(G):
                        pad_keys(f, pf, g)
                        if not dyn and i == -2 and g == 1:
                            low_part(1)

            run(pool, iteration)
            low_tokens(NB - 1)

            def chunk(c):
                for q in range(FH, HV):
                    e = q // FH
                    pool.wait_ge(hl_ok, c * HV + q - 1)
                    pool.wait_ge(wb_ok, c * NE + e)
                    pool.wait_ge(su_ok, c * HV + q + 1)
                    pool.tensor_tensor(hid[:, q % 2, :], act_up[:, q % 2, :], wrow[:, (e - 1) % 2, :],
                                       op=ALU.mult).then_inc(h_ok, 1)

            chunk(0)
            with pool.Fori(1, NCH, 1) as c:
                chunk(c)

        @block.scalar
        def _(act):
            def norm_apply(b, src, dst, r, n, ready, done):
                act.wait_ge(ready, b + 1)
                for a in range(TT):
                    last = act.activation(dst[:, a, :], src[:, a, :], ACT.Identity, bias=n[:, a:a + 1],
                                          scale=r[:, a:a + 1])
                last.then_inc(done, 1)

            def evac_heads(b, half):
                act.wait_ge(pv_ok, b * G + 2 * half + 2)
                if half == 0 and (not isinstance(b, int) or b >= 1):
                    act.wait_ge(un_ok, b * TT)
                act.activation(UT[:, 2 * half:2 * half + 2, :], ps[:, PU, :].rearrange("p (g t) -> p g t", g=2),
                               ACT.Copy).then_inc(ut_ok, 1)

            norm_apply(0, X[:, tiles(0), :], xn, rstd, nbias, rs1, xn_ok)

            def iteration(i, ph, has):
                front, _, scores, tail, gates = has
                if front:
                    f = i + 2
                    act.wait_ge(xt_ok, f + 1)
                    if not isinstance(i, int) or f >= 1:
                        act.wait_ge(v_ok, f)
                    act.activation(xnT[:, :], ps[:, PM + 1, 0:S], ACT.Copy).then_inc(xnT_ok, 1)

                def maxima_evac():
                    act.wait_ge(mt_ok, i + 1)
                    if not isinstance(i, int) or i >= 1:
                        for g in range(G):
                            act.wait_ge(sh_ok[g], 16 * i)
                    act.activation(MT[:, :], ps[0:32, PM, 0:S], ACT.Copy).then_inc(mts_ok, 1)

                def exp_head(b, pb, h):
                    n = b * H + h
                    act.wait_ge(sb_ok, n + 1)
                    if h % G == 0 and (not isinstance(b, int) or n >= 8):
                        act.wait_ge(pv_ok, b * G + h // G - 1)
                    act.activation(PR[:, h % 8, :, :],
                                   ps[:, SB + (pb + h) % 3, :].rearrange("p (a t) -> p a t", a=TT),
                                   ACT.Exp, scale=SCALE).then_inc(ex_ok, 1)

                def hi_part():
                    f = i + 2
                    act.wait_ge(rot_ok, f + 1)
                    if not isinstance(i, int) or f >= 1:
                        for g in range(G):
                            act.wait_ge(qk_ok[g], 16 * STACKS * f)
                    act.activation(HL[:, :, 0, :], rc[:, :, :], ACT.Copy).then_inc(hi_ok, 1)

                def second_norm():
                    t = i - 2
                    act.wait_ge(xt2_ok, t + 1)
                    if not isinstance(i, int) or t >= 1:
                        act.wait_ge(xl_ok, t)
                    act.activation(xf[:, :], ps[:, PM + 1, 0:S], ACT.Copy).then_inc(xf_ok, 1)
                    act.wait_ge(xf_ok, t + 1)
                    act.activation(XH[:, bass.ds(t * S, S)], xf[:, :], ACT.Copy).then_inc(xh_ok, 1)

                def gate_exp():
                    t = i - 2
                    act.wait_ge(g_ok, t + 1)
                    act.activation(GE[:, tiles(t), :], ps[:, PM, 0:TT * NE].rearrange("p (a e) -> p a e", a=TT),
                                   ACT.Exp, scale=-1.0).then_inc(ge_ok, 1)

                def att_evac():
                    t = i - 1
                    act.wait_ge(at_ok, t + 1)
                    act.activation(attT[:, :], ps[:, PM + 1, 0:S], ACT.Copy).then_inc(atT_ok, 1)

                def first_apply():
                    act.wait_ge(xt_ok, i + 3)
                    norm_apply(i + 3, X[:, tiles(i + 3), :], xn, rstd, nbias, rs1, xn_ok)

                def second_apply():
                    t = i - 2
                    if not isinstance(i, int) or t >= 1:
                        act.wait_ge(xt2_ok, t)
                    norm_apply(t, X[:, tiles(t), :], xn2, rstd2, nbias2, rs2, xn2_ok)

                more = front and (not isinstance(i, int) or i + 3 < NB)
                if isinstance(i, int) and i == -2:
                    first_apply()
                for slot in range(H):
                    if slot < J:
                        if tail:
                            exp_head(i - 1, (ph - 1) % NBUF, H - J + slot)
                    elif scores:
                        exp_head(i, ph, slot - J)
                    if slot == 0 and scores:
                        maxima_evac()
                    if slot == 5 and front:
                        hi_part()
                    if slot == 6 and tail:
                        evac_heads(i - 1, 1)
                    if slot == 8 and gates:
                        second_apply()
                    if slot == 9 and more and (not isinstance(i, int) or i != -2):
                        first_apply()
                    if slot == 11 and tail:
                        att_evac()
                    if slot == 13 and gates:
                        second_norm()
                    if slot == 15 and scores:
                        evac_heads(i, 0)
                    if slot == 15 and gates:
                        gate_exp()

            run(act, iteration)

            act.wait_ge(sb_ok, NB * H)
            act.wait_ge(pv_ok, NB * G)
            act.wait_ge(un_ok, NB * TT)

            act.activation(silu_table[:, :], halves[:, 0:1], ACT.Silu)

            def hidden_hi(c, q):
                n = c * HV + q
                if not isinstance(n, int) or n >= 3:
                    act.wait_ge(dn_ok, n - 2)
                if q < FH:
                    act.wait_ge(su_ok, n + 1)
                else:
                    act.wait_ge(h_ok, c * NE * FH + q - FH + 1)
                act.activation(hid_part[:, q % 3, 0, :], hid[:, q % 2, :], ACT.Copy).then_inc(hh_ok, 1)

            def sum_out(c):
                if not isinstance(c, int) or c >= 1:
                    act.wait_ge(y_t, c)
                act.wait_ge(dn_ok, c * HV + HV)
                act.activation(yT, ps[:, Y0, :], ACT.Copy).then_inc(yT_ok, 1)

            def chunk(c):
                dyn = not isinstance(c, int)
                for q in range(HV):
                    n = c * HV + q
                    if dyn or n >= 2:
                        act.wait_ge(su_ok, n - 1)
                    act.wait_ge(gu_ok, n + 1)
                    act.activation(silu[:, q % 2, :], ps[:, G0 + q % 2, :], ACT.Silu).then_inc(si_ok, 1)
                    if q:
                        hidden_hi(c, q - 1)
                    elif dyn or c >= 1:
                        hidden_hi(c - 1, HV - 1)
                    if q % 2 and q // 2 < NE:
                        e = q // 2 + 1
                        m = c * NE + e
                        if dyn or m >= 3:
                            act.wait_ge(h_ok, (m - 2) * FH)
                        act.wait_ge(wb_t, m)
                        act.activation(wrow[:, (e - 1) % 2, :], ps[:, wrow_bank(e), :], ACT.Copy).then_inc(wb_ok, 1)
                    if q == LAG - 1 and (dyn or c >= 1):
                        sum_out(c - 1)

            chunk(0)
            with act.Fori(1, NCH, 1) as c:
                chunk(c)
            hidden_hi(NCH - 1, HV - 1)
            sum_out(NCH - 1)

        @block.vector
        def _(dve):
            dve.memset(halves[:, :], -0.5).then_inc(setup_dve, 1)

            def norm_stats(src, st, s_st):
                for a in range(TT):
                    last = dve.bn_stats(st[:, a, :], src[:, a, :])
                last.then_inc(s_st, 1)

            def norm_mean(b, st, m, v, n, s_mv, done):
                for a in range(TT):
                    last = dve.bn_aggr(m[:, a, :], st[:, a, :])
                last.then_inc(s_mv, 1)
                dve.wait_ge(s_mv, b + 1)
                dve.tensor_scalar(v[:, :], m[:, :, 1:2].rearrange("p a o -> p (a o)"), EPS, None, ALU.add)
                dve.tensor_scalar(n[:, :], m[:, :, 0:1].rearrange("p a o -> p (a o)"), -1.0, None,
                                  ALU.mult).then_inc(done, 1)

            dve.wait_ge(xld[0], 16)
            norm_stats(X[:, tiles(0), :], stat, st1)
            dve.wait_ge(st1, 1)
            norm_mean(0, stat, mv, veps, nmean, mv1, ve1)
            for n in range(NBUF):
                dve.memset(QK[KA:P, n, 1, :, :].bitcast(F32), 1.0).then_inc(setup_dve, 1)
            dve.wait_ge(cst_ld, 16)
            dve.wait_ge(bcol_ld, 16)

            ROUTED = 20
            steps = [0]

            def step(ins):
                steps[0] += 1
                ins.then_inc(rt, 1)
                dve.wait_ge(rt, steps[0])

            def route(t0, t1):
                n = t1 - t0
                gate, rank, wsel, wpart, beats, beats_flat = routing_tiles(n)
                wsum, wrec = GE[:, t0:t1, 0:1], GE[:, t0:t1, 1:2]
                dve.wait_ge(ge_ok, t1 // TT)
                step(dve.tensor_scalar(gate, GE[:, t0:t1, :], 1.0, None, ALU.add))
                step(dve.reciprocal(gate, gate))
                dve.memset(beats_flat[:, :, 0:NE * NE:NE + 1], 0.0)
                for j in range(NE):
                    for e0, e1, op in ((0, j, ALU.is_gt), (j + 1, NE, ALU.is_ge)):
                        if e0 < e1:
                            last = dve.tensor_tensor(beats[:, :, e0:e1, j], gate[:, :, j:j + 1].broadcast_to([P, n, e1 - e0]),
                                                     gate[:, :, e0:e1], op=op)
                step(last)
                step(dve.tensor_reduce(rank, beats, op=ALU.add, axis=AX.X))
                step(dve.scalar_tensor_tensor(wsel, rank, 2.0, gate, op0=ALU.is_lt, op1=ALU.mult))
                step(dve.tensor_reduce(wsum, wsel, op=ALU.add, axis=AX.X))
                step(dve.reciprocal(wrec, wsum))
                step(dve.scalar_tensor_tensor(wpart, wsel, 1.0 / 3.0, wrec.broadcast_to([P, n, NE]),
                                              op0=ALU.mult, op1=ALU.mult))
                step(dve.tensor_copy(WHL[:, t0:t1, 0, :], wpart))
                step(dve.tensor_tensor(WHL[:, t0:t1, 1, :], wpart, WHL[:, t0:t1, 0, :].bitcast(F32), op=ALU.subtract))

            def chunk_weights(c):
                dve.tensor_copy(WC[:, :, :], WHL[:, bass.ds(c * CT, CT), :, :].rearrange("p t l e -> p t (l e)")
                                .bitcast(F32)).then_inc(wc_ok, 1)

            def iteration(i, ph, has):
                front, maxima, scores, tail, gates = has
                more = not isinstance(i, int) or i + 4 < NB

                def reduce(u):
                    if not maxima:
                        return
                    a = i + 1
                    if u == 0 and (not isinstance(i, int) or a >= 1):
                        dve.wait_ge(ml_ok, a)
                    dve.wait_ge(sa_ok, a * H + u + 1)
                    hp, qt = u // 2, u % 2
                    dve.tensor_reduce(MX[:, qt, 2 * hp:2 * hp + 2],
                                      ps[:, SA + u % 2, :].rearrange("p (h k) -> p h k", h=2),
                                      op=ALU.max, axis=AX.X).then_inc(mx_ok, 1)

                def rope_mul(n, wait, bank_, done):
                    f = i + 2
                    dve.wait_ge(wait, f + 1)
                    if n == 0 and (not isinstance(i, int) or f >= 1):
                        dve.wait_ge(lo_ok, f)
                    dve.scalar_tensor_tensor(rc[:, n, :], ps[:, PM + bank_, 0:S], bcol[:, 2 * n:2 * n + 1],
                                             rope[:, 0, :], op0=ALU.add, op1=ALU.mult)
                    dve.scalar_tensor_tensor(rs[:, n, :], ps[:, PM + bank_, S:2 * S], bcol[:, 2 * n + 1:2 * n + 2],
                                             rope[:, 1, :], op0=ALU.add, op1=ALU.mult).then_inc(done, 1)

                def values():
                    f, pf = i + 2, (ph + 2) % NBUF
                    if isinstance(i, int) and f == 0:
                        dve.wait_ge(ld, 16 * NLD)
                        dve.wait_ge(setup_pool, 2)
                    dve.wait_ge(v_ok, f + 1)
                    if not isinstance(i, int) or i >= 1:
                        dve.wait_ge(pv_ok, i * G)
                    dve.tensor_tensor(VX[:, pf, :, :, 0:DH],
                                      ps[:, PM, 0:S].rearrange("p (a h d) -> p a h d", a=TT, h=H),
                                      brow[:, 0:1, :].rearrange("p o (h d) -> p o h d", h=H)
                                      .broadcast_to([P, TT, H, DH]), op=ALU.add).then_inc(vx_ok, 1)

                def statistics(b):
                    if isinstance(i, int) and i < 0:
                        for n in range(1 if b == 1 else b, 2 if b == 1 else b + 1):
                            dve.wait_ge(xld[n], 16)
                    norm_stats(X[:, tiles(b), :], stat, st1)
                    dve.wait_ge(st1, b + 1)
                    dve.wait_ge(rs1, b)

                def means(b):
                    norm_mean(b, stat, mv, veps, nmean, mv1, ve1)

                def normalise(a):
                    t = i - 1
                    bk_ = PM + 1 - a
                    u = ps[:, bk_, :].rearrange("p (h c) -> p h c", h=H)
                    dve.wait_ge(un_ok, t * TT + a + 1)
                    dve.reciprocal(rden[:, a, :], u[:, :, DH:DH + 1].rearrange("p h o -> p (h o)")).then_inc(rd_ok, 1)
                    dve.wait_ge(rd_ok, t * TT + a + 1)
                    if a == 0 and (not isinstance(i, int) or t >= 1):
                        dve.wait_ge(at_ok, t)
                    dve.tensor_tensor(att[:, a, :].rearrange("p (h d) -> p h d", h=H), u[:, :, 0:DH],
                                      rden[:, a, :].rearrange("p (h o) -> p h o", o=1).broadcast_to([P, H, DH]),
                                      op=ALU.mult).then_inc(att_ok, 1)

                def residual():
                    t = i - 1
                    dve.wait_ge(wo_ok, t + 1)
                    dve.wait_ge(bo_ok, t + 1)
                    dve.tensor_tensor(X[:, tiles(t), :], ps[:, PM, 0:S].rearrange("p (a d) -> p a d", a=TT),
                                      X[:, tiles(t), :], op=ALU.add).then_inc(x2_ok, 1)

                def split_maxima():
                    a = i + 1
                    if tail:
                        dve.wait_ge(x2_ok, i)
                    if maxima:
                        dve.wait_ge(mx_ok, a * H + H)
                        if not isinstance(i, int) or a >= 1:
                            dve.wait_ge(mt_ok, a)
                        m = MX[:, :, :].rearrange("p a (g j) -> p a g j", g=G)
                        dve.tensor_scalar(MHL[:, :, :, 0, :], m, -1.0, None, ALU.mult).then_inc(mh_ok, 1)
                        dve.wait_ge(mh_ok, a + 1)
                        for qt in range(TT):
                            last = dve.scalar_tensor_tensor(
                                MHL[:, qt, :, 1, :], m[:, qt, :, :], -1.0, MHL[:, qt, :, 0, :].bitcast(F32),
                                op0=ALU.mult, op1=ALU.subtract)
                        last.then_inc(ml_ok, 1)

                if scores:
                    reduce(0)
                if isinstance(i, int) and i == NB:
                    dve.wait_ge(pv_ok, (NB - 1) * G)
                    route(0, ROUTED)
                if isinstance(i, int) and i == NB + 1:
                    dve.wait_ge(sb_ok, NB * H)
                    dve.tensor_tensor(SEL, ident[0:2 * NE, 0:NE].rearrange("p (e o) -> p e o", o=1)
                                      .broadcast_to([2 * NE, NE, P]),
                                      ident[0:2 * NE, NE:2 * NE].rearrange("p (e o) -> p e o", o=1)
                                      .broadcast_to([2 * NE, NE, P]), op=ALU.add).then_inc(sel_ok, 1)
                front_first = front and not scores
                if isinstance(i, int) and i == -2:
                    statistics(1)
                    means(1)
                if front_first:
                    rope_mul(0, q_ok, 0, rq_ok)
                    rope_mul(1, k_ok, 1, rk_ok)
                    values()
                    reduce(0)
                if gates:
                    dve.wait_ge(st2, i - 1)
                    if not isinstance(i, int) or i >= 3:
                        dve.wait_ge(rs2, i - 2)
                reduce(1)
                if gates:
                    norm_mean(i - 2, stat2, mv2, veps2, nmean2, mvs2, ve2)
                reduce(2); reduce(3)
                if front and not front_first:
                    rope_mul(0, q_ok, 0, rq_ok)
                reduce(4)
                if front and not front_first:
                    rope_mul(1, k_ok, 1, rk_ok)
                reduce(5); reduce(6); reduce(7)
                if front and not front_first:
                    values()
                reduce(8); reduce(9)
                if tail:
                    normalise(0)
                reduce(10)
                if tail:
                    normalise(1)
                reduce(11)
                if isinstance(i, int) and i == NB + 1:
                    chunk_weights(0)
                    route(ROUTED, NT - TT)
                reduce(12)
                if more:
                    statistics(i + 4)
                reduce(13)
                if more:
                    means(i + 4)
                if tail:
                    residual()
                reduce(14)
                reduce(15)
                split_maxima()
                if tail:
                    norm_stats(X[:, tiles(i - 1), :], stat2, st2)

            run(dve, iteration)

            def hidden_lo(n, q):
                dve.wait_ge(hh_ok, n + 1)
                dve.tensor_tensor(hid_part[:, q % 3, 1, :], hid[:, q % 2, :], hid_part[:, q % 3, 0, :].bitcast(F32),
                                  op=ALU.subtract).then_inc(hl_ok, 1)

            def residual(c):
                dve.wait_ge(y_t, c + 1)
                rows = X[:, bass.ds(c * CT, CT), :]
                dve.tensor_tensor(rows, ps[:, M0 + 1, :].rearrange("p (a d) -> p a d", a=CT), rows,
                                  op=ALU.add).then_inc(y_ok, 1)

            def chunk(c):
                dyn = not isinstance(c, int)
                if dyn or c >= 1:
                    dve.wait_ge(wt_t, c)
                    chunk_weights(c)
                for q in range(HV):
                    n = c * HV + q
                    dve.wait_ge(si_ok, n + 1)
                    if q < FH:
                        if dyn or n >= 2:
                            dve.wait_ge(hl_ok, n - 1)
                        dve.scalar_tensor_tensor(hid[:, q % 2, :], silu[:, q % 2, :], 1.0 / 3.0, ps[:, U0 + q % 2, :],
                                                 op0=ALU.mult, op1=ALU.mult).then_inc(su_ok, 1)
                    else:
                        if dyn or c * NE + q >= 2 * FH:
                            dve.wait_ge(h_ok, c * NE * FH + q - 2 * FH + 1 if q >= 2 * FH else c * NE * FH)
                        dve.tensor_tensor(act_up[:, q % 2, :], silu[:, q % 2, :], ps[:, U0 + q % 2, :],
                                          op=ALU.mult).then_inc(su_ok, 1)
                    if dyn or n >= 1:
                        hidden_lo(n - 1, (q - 1) % HV)
                    if q == 1 and not dyn and c == 0:
                        route(NT - TT, NT)
                    if q == 0:
                        if dyn or c >= 1:
                            dve.wait_ge(wb_t, c * NE)
                        dve.wait_ge(wt_t, c + 1)
                        dve.tensor_copy(WT, ps[0:2 * NE, M0, :]).then_inc(wt_ok, 1)
                    if q == 5 and (dyn or c >= 1):
                        residual(c - 1)

            chunk(0)
            with dve.Fori(1, NCH, 1) as c:
                chunk(c)
            hidden_lo(NCH * HV - 1, HV - 1)
            residual(NCH - 1)

        @block.tensor
        def _(pe):
            mm = pe.matmul
            pe.wait_ge(cst_ld, 16)

            def up(c, q):
                dyn = not isinstance(c, int)
                n = c * HV + q
                e, v = q // FH, q % FH
                if not dyn and c == 0:
                    pe.wait_ge(wl_ok, e + 1)
                if dyn or n >= 2:
                    pe.wait_ge(su_ok, n - 1)
                tok = bass.ds(c * CH, CH)
                for b, w in ((G0, v * P), (U0, F + v * P)):
                    for k, (l, part) in enumerate(((0, XH), (0, XL), (1, XH))):
                        last = mm(ps[:, b + q % 2, :], up_part(e, l)[:, w:w + P], part[:, tok],
                                  start=k == 0, stop=k == 2)
                last.then_inc(gu_ok, 1)

            def heads_out(b, pb, g):
                dyn = not isinstance(b, int)
                pe.wait_ge(ex_ok, b * H + 4 * g + 4)
                if g == 0:
                    pe.wait_ge(vx_ok, b + 1)
                    if dyn or b >= 1:
                        pe.wait_ge(ut_ok, b * 2)
                if g == 2:
                    pe.wait_ge(ut_ok, b * 2 + 1)
                for kt in range(TT):
                    for j in range(J):
                        last = mm(ps[32 * j:32 * j + 32, PU, (g % 2) * S:(g % 2 + 1) * S],
                                  VX[:, pb, kt, G * g + j, :], PR[:, (G * g + j) % 8, kt, :],
                                  start=kt == 0, stop=kt == TT - 1)
                last.then_inc(pv_ok, 1)

            def iteration(i, ph, has):
                front, maxima, scores, tail, gates = has
                dyn = not isinstance(i, int)
                f, t, gt = i + 2, i - 1, i - 2
                pa = (ph + 1) % NBUF

                def unit(u):
                    if not maxima:
                        return
                    a = i + 1
                    if u % G == 0:
                        pe.wait_ge(kz_ok, a * G + u // G + 1)
                    n = a * H + u
                    if dyn or n >= 2:
                        pe.wait_ge(mx_ok, n - 1)
                    hp, qt = u // 2, u % 2
                    g, j = hp // 2, 2 * (hp % 2)
                    mm(ps[:, SA + u % 2, :], QK[0:KA, pa, 0, g, qt * P:(qt + 1) * P],
                       KZ[0:KA, pa, g, j:j + 2, :], start=True, stop=True).then_inc(sa_ok, 1)

                def head(slot):
                    if not (tail if slot < J else scores):
                        return
                    b, h = (t, H - J + slot) if slot < J else (i, slot - J)
                    pb = (ph - 1) % NBUF if slot < J else ph
                    n = b * H + h
                    if h % J == 0:
                        pe.wait_ge(sh_ok[h // J], (b + 1) * 16)
                    if dyn or n >= 3:
                        pe.wait_ge(ex_ok, n - 2)
                    g, j = h // J, h % J
                    for kt in range(TT):
                        last = mm(ps[:, SB + (pb + h) % 3, kt * S:(kt + 1) * S],
                                  KZ[0:KB, pb, g, j, kt * P:(kt + 1) * P], QK[0:KB, pb, 0, g, :],
                                  start=True, stop=True)
                    last.then_inc(sb_ok, 1)

                def project(n, bank_, done):
                    for s, w in enumerate((wraw[:, 2 * n, :], wraw[:, 2 * n + 1, :])):
                        last = mm(ps[:, PM + bank_, s * S:(s + 1) * S], w, xnT[:, :], start=True, stop=True)
                    last.then_inc(done, 1)

                def back_to_rows(a, bank_):
                    for g in range(G):
                        last = pe.transpose(ps[:, PM + bank_, g * P:(g + 1) * P], UT[:, g, a * P:(a + 1) * P], ident)
                    last.then_inc(un_ok, 1)

                def maxima_rows():
                    if not scores:
                        return
                    pe.wait_ge(ml_ok, i + 1)
                    if dyn or i >= 3:
                        pe.wait_ge(ge_ok, i - 2)
                    elif i == 2:
                        pe.wait_ge(x2_ok, i - 1)
                    else:
                        pe.wait_ge(vx_ok, i + 2)
                    for a in range(TT):
                        last = pe.transpose(ps[0:32, PM, a * P:(a + 1) * P],
                                            MHL[:, a, :, :, :].rearrange("p g l j -> p (g l j)").bitcast(F32), ident)
                    last.then_inc(mt_ok, 1)

                def front_tokens():
                    if not front:
                        return
                    pe.wait_ge(xn_ok, f + 1)
                    if dyn or i >= 3:
                        pe.wait_ge(xf_ok, i - 2)
                    elif i == 2:
                        pe.wait_ge(atT_ok, i - 1)
                    elif i >= -1:
                        pe.wait_ge(rk_ok, f)
                    for a in range(TT):
                        last = pe.transpose(ps[:, PM + 1, a * P:(a + 1) * P], xn[:, a, :], ident)
                    last.then_inc(xt_ok, 1)

                def queries():
                    if not front:
                        return
                    pe.wait_ge(xnT_ok, f + 1)
                    if isinstance(i, int) and i == -2:
                        pe.wait_ge(wqk_ld, 16)
                    if scores:
                        pe.wait_ge(mts_ok, i + 1)
                    elif i == -1:
                        pe.wait_ge(vx_ok, f)
                    project(0, 0, q_ok)

                def keys():
                    if front:
                        project(1, 1, k_ok)

                def values():
                    if not front:
                        return
                    if isinstance(i, int) and i == -2:
                        pe.wait_ge(ld, 16 * NLD)
                    pe.wait_ge(rq_ok, f + 1)
                    for a in range(TT):
                        last = mm(ps[:, PM, a * P:(a + 1) * P], xnT[:, a * P:(a + 1) * P], wraw[:, 4, :],
                                  start=True, stop=True)
                    last.then_inc(v_ok, 1)

                def rows_0():
                    if not tail:
                        return
                    pe.wait_ge(ut_ok, t * 2 + 2)
                    if front:
                        pe.wait_ge(rk_ok, f + 1)
                    else:
                        pe.wait_ge(xf_ok, gt)
                    back_to_rows(0, 1)

                def rows_1():
                    if not tail:
                        return
                    if front:
                        pe.wait_ge(vx_ok, f + 1)
                    elif scores:
                        pe.wait_ge(mts_ok, i + 1)
                    else:
                        pe.wait_ge(ge_ok, gt)
                    back_to_rows(1, 0)

                def attention_T():
                    if not tail:
                        return
                    pe.wait_ge(att_ok, t * TT + TT)
                    for a in range(TT):
                        last = pe.transpose(ps[:, PM + 1, a * P:(a + 1) * P], att[:, a, :], ident)
                    last.then_inc(at_ok, 1)

                def output():
                    if not tail:
                        return
                    pe.wait_ge(atT_ok, t + 1)
                    for a in range(TT):
                        last = mm(ps[:, PM, a * P:(a + 1) * P], attT[:, a * P:(a + 1) * P], wraw[:, 5, :],
                                  start=True, stop=True)
                    last.then_inc(wo_ok, 1)

                def second_tokens():
                    if not gates:
                        return
                    pe.wait_ge(xn2_ok, gt + 1)
                    if tail:
                        pe.wait_ge(atT_ok, t + 1)
                    else:
                        pe.wait_ge(xf_ok, gt)
                    for a in range(TT):
                        last = pe.transpose(ps[:, PM + 1, a * P:(a + 1) * P], xn2[:, a, :], ident)
                    last.then_inc(xt2_ok, 1)

                def gate_logits():
                    if not gates:
                        return
                    pe.wait_ge(xf_ok, gt + 1)
                    if tail:
                        pe.wait_ge(x2_ok, t + 1)
                    else:
                        pe.wait_ge(ge_ok, gt)
                    for a in range(TT):
                        last = mm(ps[:, PM, a * NE:(a + 1) * NE], xf[:, a * P:(a + 1) * P], wg[:, :],
                                  start=True, stop=True)
                    last.then_inc(g_ok, 1)

                def heads(g):
                    if g >= 2 and tail:
                        heads_out(t, (ph - 1) % NBUF, g)
                    elif g < 2 and scores:
                        heads_out(i, ph, g)

                if isinstance(i, int) and i == NB + 1:
                    pe.wait_ge(ex_ok, NB * H)
                    pe.wait_ge(xl_ok, CH // S)
                    for q in range(FH):
                        up(0, q)

                if not scores:
                    front_tokens(); queries(); keys(); values()
                unit(0); head(0)
                if scores:
                    front_tokens()
                unit(1); head(1); maxima_rows(); heads(2)
                unit(2); head(2); unit(3)
                if scores:
                    queries()
                head(3); unit(4)
                if scores:
                    keys()
                head(4)
                if scores:
                    values()
                unit(5); head(5)
                unit(6); head(6)
                unit(7); heads(3); head(7)
                unit(8); head(8)
                unit(9); head(9); rows_0()
                unit(10); head(10); rows_1()
                unit(11); heads(0); head(11)
                unit(12); attention_T(); head(12)
                unit(13); head(13); output(); second_tokens()
                unit(14); head(14)
                unit(15); heads(1); head(15); gate_logits()

            run(pe, iteration)

            pe.wait_ge(sel_ok, 1)
            pe.wait_ge(xl_ok, NB)
            pe.wait_ge(ge_ok, NB)
            pe.wait_ge(ut_ok, NB * 2)

            def down(c, q):
                e, v = q // FH, q % FH
                if q == 0 and (not isinstance(c, int) or c >= 1):
                    pe.wait_ge(yT_ok, c)
                pe.wait_ge(hl_ok, c * HV + q + 1)
                for k, (l, m) in enumerate(((0, 0), (0, 1), (1, 0))):
                    last = mm(ps[:, Y0, :], dn_part(e, l)[:, v, :], hid_part[:, q % 3, m, :],
                              start=q == 0 and k == 0, stop=q == HV - 1 and k == 2)
                last.then_inc(dn_ok, 1)

            def sum_rows(c):
                pe.wait_ge(yT_ok, c + 1)
                for a in range(CT):
                    last = pe.transpose(ps[:, M0 + 1, a * P:(a + 1) * P], yT[:, a * P:(a + 1) * P], ident)
                last.then_inc(y_t, 1)

            def chunk(c):
                dyn = not isinstance(c, int)
                for k in range(NEX):
                    for q in (2 * k, 2 * k + 1):
                        if dyn or c >= 1 or q >= FH:
                            up(c, q)
                        if q >= LAG:
                            down(c, q - LAG)
                        elif dyn or c >= 1:
                            down(c - 1, HV - LAG + q)
                        if q == 0:
                            if dyn or c >= 1:
                                pe.wait_ge(wb_ok, c * NE - 1)
                            pe.wait_ge(wc_ok, c + 1)
                            for a in range(CT):
                                last = pe.transpose(ps[0:2 * NE, M0, a * P:(a + 1) * P], WC[:, a, :], ident)
                            last.then_inc(wt_t, 1)
                    e = k + 1
                    if e <= NE:
                        if e == 1:
                            pe.wait_ge(wt_ok, c + 1)
                            if dyn or c >= 1:
                                pe.wait_ge(wb_ok, c * NE)
                        elif e == 3:
                            pe.wait_ge(wb_ok, c * NE + 2)
                        elif e == 4 and (dyn or c >= 1):
                            pe.wait_ge(y_ok, c)
                        elif e >= 4:
                            pe.wait_ge(wb_ok, c * NE + e - 2)
                        mm(ps[:, wrow_bank(e), :], SEL[:, e - 1, :], WT, start=True, stop=True).then_inc(wb_t, 1)
                    if k == 1 and (dyn or c >= 1):
                        pe.wait_ge(wb_ok, c * NE + 1)
                        sum_rows(c - 1)

            chunk(0)
            with pe.Fori(1, NCH, 1) as c:
                chunk(c)
            for q in range(HV - LAG, HV):
                down(NCH - 1, q)
            sum_rows(NCH - 1)


def constants():
    import numpy as np
    c = np.zeros((P, C_ALL), np.float32)
    inv_freq = (1.0 / 10000.0 ** (np.arange(0, DH, 2, dtype=np.float32) / np.float32(DH))).astype(np.float32)
    freqs = np.arange(S, dtype=np.float32)[:, None] * inv_freq[None, :]
    ang = np.concatenate((freqs, freqs), axis=-1)[:, ::2].astype(np.float32)
    for p in range(P):
        a = ang[:, (p % DH) // 2]
        c[p, C_ROPE:C_ROPE + S] = np.cos(a)
        c[p, C_ROPE + S:C_ROPE + 2 * S] = np.sin(a) if p % 2 else -np.sin(a)
        c[p, C_IDENT + p] = 1.0
        if p < KA:
            c[p, C_MASK + p % 32 // DH] = 1.0
        elif p < KB:
            c[p, C_MASK + p % J] = 1.0
    return c


def kernel(L0_attn_x, L0_attn_Wq, L0_attn_bq, L0_attn_Wk, L0_attn_bk, L0_attn_Wv, L0_attn_bv, L0_attn_Wo, L0_attn_bo,
           L0_ffn_Wg, L0_ffn_Ws1, L0_ffn_Ws3, L0_ffn_Ws2, L0_ffn_We1, L0_ffn_We3, L0_ffn_We2):
    import numpy as np
    import concourse.bacc as bacc
    from concourse.bass_utils import run_bass_kernel_spmd

    def swapped(a):
        a = np.asarray(a)
        return a.reshape(a.shape[:-1] + (a.shape[-1] // 2, 2))[..., ::-1].reshape(a.shape)

    w_att = np.concatenate([np.asarray(L0_attn_Wq), swapped(L0_attn_Wq), np.asarray(L0_attn_Wk),
                            swapped(L0_attn_Wk), np.asarray(L0_attn_Wv), np.asarray(L0_attn_Wo)], axis=1)
    b_cols = np.stack([np.asarray(L0_attn_bq), swapped(L0_attn_bq), np.asarray(L0_attn_bk), swapped(L0_attn_bk)], axis=1)
    w1 = np.concatenate([np.asarray(L0_ffn_Ws1)[None], np.asarray(L0_ffn_We1)])
    w3 = np.concatenate([np.asarray(L0_ffn_Ws3)[None], np.asarray(L0_ffn_We3)])
    w2 = np.concatenate([np.asarray(L0_ffn_Ws2)[None], np.asarray(L0_ffn_We2)])
    w_up = np.concatenate([w1, w3], axis=2).transpose(1, 0, 2)
    w_down = w2.reshape(NEX, FH, P, D).transpose(2, 0, 1, 3)

    nc = bacc.Bacc("TRN2", target_bir_lowering=False, num_devices=1)
    arrays, args = {}, []
    for name, a in (("x", L0_attn_x), ("w_att", w_att), ("b_cols", b_cols), ("bv", L0_attn_bv), ("bo", L0_attn_bo),
                    ("Wg", L0_ffn_Wg), ("w_up", w_up), ("w_down", w_down), ("const", constants())):
        a = np.ascontiguousarray(a)
        arrays[f"in_{name}"] = a
        args.append(nc.dram_tensor(f"in_{name}", a.shape, mybir.dt.from_np(a.dtype), kind="ExternalInput").ap())
    args.append(nc.dram_tensor("out_0", (NB, S, D), F32, kind="ExternalOutput").ap())
    layer_kernel(nc, *args)
    r = run_bass_kernel_spmd(nc, [arrays], core_ids=[0])
    return r.results[0]["out_0"]
```
